# Optimizing a Trainium2 kernel written in Bass

```python
import numpy as np
import jax
import jax.numpy as jnp

def _softmax(x, axis=-1):
    return jax.nn.softmax(x, axis=axis)

def _gelu(x):
    return jax.nn.gelu(x, approximate=True)

def _silu(x):
    return jax.nn.silu(x)

def _sigmoid(x):
    return jax.nn.sigmoid(x)

def _layernorm(x, axis=-1, eps=1e-05):
    m = jnp.mean(x, axis=axis, keepdims=True)
    v = jnp.var(x, axis=axis, keepdims=True)
    return (x - m) / jnp.sqrt(v + eps)

def _scatter_add(tgt, idx, src, axis=0):
    return tgt.at[idx].add(src)

def _segment_sum(src, seg, n):
    return jax.ops.segment_sum(src, seg, n)
kernel_name = 'mk_decoder_postln_d1_seqx_r8_25c900'

def setup_inputs(seed: int=0):
    np.random.seed(seed)
    _w = jnp.asarray

    def _rec_inputs():
        import jax
        import jax.numpy as jnp
        _rk = jax.random.key(seed)
        x = -0.0002928 + 1 * jax.random.normal(jax.random.fold_in(_rk, 1), (8, 256, 256), jnp.float32)
        _lenS = 256 - jax.random.randint(jax.random.fold_in(_rk, 7), (8,), 0, max(1, 256 // 4) + 1, jnp.int32)
        _lenS2 = 64 - jax.random.randint(jax.random.fold_in(_rk, 8), (8,), 0, max(1, 64 // 4) + 1, jnp.int32)
        _ctx_512P = jax.random.normal(jax.random.fold_in(_rk, 11), (8, 16, 64), jnp.float32)
        _ctx_512c = jax.random.dirichlet(jax.random.fold_in(_rk, 511), 0.3 * jnp.ones((16,), jnp.float32), (8, 64))
        _ctx_512t = jnp.einsum('bsk,bkd->bsd', _ctx_512c, _ctx_512P)
        _ctx_512t = _ctx_512t * jax.lax.rsqrt(jnp.mean(jnp.square(_ctx_512t)) + 1e-12) * 0.953939
        ctx_512 = 0.000227908 + 0.99994 * (_ctx_512t + 0.3 * jax.random.normal(jax.random.fold_in(_rk, 611), (8, 64, 64), jnp.float32))
        return (x, ctx_512)
    x, ctx_512 = _rec_inputs()

    def _L0_attn_setup():
        import jax, jax.numpy as jnp
        import numpy as np
        import math
        B, T, D = (4, 512, 256)
        H = 16
        HD = D // H
        L = 64
        K_TOP = 4
        key = jax.random.key(seed)
        ks = jax.random.split(key, 10)
        lim = 1.0 / math.sqrt(D)
        u = lambda k, shape: jax.random.uniform(k, shape, jnp.float32, -lim, lim)
        return {'hidden_states': jax.random.normal(ks[0], (B, T, D), jnp.float32), 'Wq': u(ks[1], (D, D)), 'bq': u(ks[2], (D,)), 'Wk': u(ks[3], (D, D)), 'bk': u(ks[4], (D,)), 'Wv': u(ks[5], (D, D)), 'bv': u(ks[6], (D,)), 'Wo': u(ks[7], (D, D)), 'bo': u(ks[8], (D,)), 'latent_keys': jax.random.normal(ks[9], (L, D), jnp.float32) * 0.1}
    _L0_attn_all = _L0_attn_setup()
    _L0_attn_in = {k: v for k, v in _L0_attn_all.items() if k in ('Wq', 'bq', 'Wk', 'bk', 'Wv', 'bv', 'Wo', 'bo', 'latent_keys')}
    del _L0_attn_all

    def _L0_xattn_setup():
        import jax, jax.numpy as jnp
        import numpy as np
        B, S, L = (2, 128, 128)
        DIM_Q, H, K, D_C, D_CQ, R = (256, 16, 128, 64, 192, 64)

        def _rope_tables(seq_len, dim, dtype):
            inv_freq = 1.0 / 10000.0 ** (jnp.arange(0, dim, 2, dtype=dtype) / dim)
            t = jnp.arange(seq_len, dtype=dtype)
            freqs = t[:, None] * inv_freq[None, :]
            sin = jnp.repeat(jnp.sin(freqs), 2, axis=-1)
            cos = jnp.repeat(jnp.cos(freqs), 2, axis=-1)
            return (sin, cos)

        def _rotate_half(x):
            h = x.shape[-1] // 2
            return jnp.concatenate([-x[..., h:], x[..., :h]], axis=-1)
        key = jax.random.key(seed)
        ks = jax.random.split(key, 8)
        s_in = 1.0 / np.sqrt(DIM_Q)
        s_k = 1.0 / np.sqrt(K)
        s_cq = 1.0 / np.sqrt(D_CQ)
        s_c = 1.0 / np.sqrt(D_C)
        return {'hidden_q': jax.random.normal(ks[0], (B, S, DIM_Q), jnp.float32), 'kv_c': jax.random.normal(ks[1], (B, L, D_C), jnp.float32), 'Wq': jax.random.normal(ks[2], (H * K, DIM_Q), jnp.float32) * s_in, 'w_kc_q': jax.random.normal(ks[3], (H, K, D_CQ), jnp.float32) * s_k, 'w_kc_kv': jax.random.normal(ks[4], (H, K, D_C), jnp.float32) * s_k, 'W_qr': jax.random.normal(ks[5], (H, D_CQ, R), jnp.float32) * s_cq / np.sqrt(R), 'W_kr': jax.random.normal(ks[6], (H, D_C, R), jnp.float32) * s_c, 'Wo': jax.random.normal(ks[7], (DIM_Q, H * K), jnp.float32) * s_k}
    _L0_xattn_all = _L0_xattn_setup()
    _L0_xattn_in = {k: v for k, v in _L0_xattn_all.items() if k in ('Wq', 'w_kc_q', 'w_kc_kv', 'W_qr', 'W_kr', 'Wo')}
    del _L0_xattn_all

    def _L0_ffn_setup():
        import jax, jax.numpy as jnp
        import numpy as np
        EPS = 1e-08

        def _rmsnorm(x, g):
            return g * (x * jax.lax.rsqrt(jnp.mean(x * x, axis=-1, keepdims=True) + EPS))

        def _act_quant(x):
            scale = 127.0 / jnp.clip(jnp.max(jnp.abs(x), axis=-1, keepdims=True), 0.0001, None)
            y = jnp.clip(jnp.round(x * scale), -128, 127) / scale
            return x + jax.lax.stop_gradient(y - x)

        def _ternary_quant(w):
            s = jnp.mean(jnp.abs(w))
            wq = jnp.round(jnp.tanh(w / (s + EPS))) * jnp.arctanh(s)
            return w + jax.lax.stop_gradient(wq - w)

        def _linear_bit(x, w, g):
            xq = _act_quant(_rmsnorm(x, g))
            wq = _ternary_quant(w)
            return jnp.einsum('bsd,od->bso', xq, wq)
        key = jax.random.key(seed)
        k = jax.random.split(key, 4)
        B, S, D, H = (4, 256, 256, 1024)
        std_up = float(np.sqrt(2.0 / (D + H)))
        std_dn = float(np.sqrt(2.0 / (H + D)))
        return {'x': jax.random.normal(k[0], (B, S, D), dtype=jnp.float32), 'w1': jax.random.normal(k[1], (H, D), dtype=jnp.float32) * std_up, 'g1': jnp.ones((D,), dtype=jnp.float32), 'w2': jax.random.normal(k[2], (H, D), dtype=jnp.float32) * std_up, 'g2': jnp.ones((D,), dtype=jnp.float32), 'w3': jax.random.normal(k[3], (D, H), dtype=jnp.float32) * std_dn, 'g3': jnp.ones((H,), dtype=jnp.float32)}
    _L0_ffn_all = _L0_ffn_setup()
    _L0_ffn_in = {k: v for k, v in _L0_ffn_all.items() if k in ('w1', 'g1', 'w2', 'g2', 'w3', 'g3')}
    del _L0_ffn_all
    return {'x': x, 'ctx_512': ctx_512, 'L0_attn_Wq': _L0_attn_in['Wq'], 'L0_attn_bq': _L0_attn_in['bq'], 'L0_attn_Wk': _L0_attn_in['Wk'], 'L0_attn_bk': _L0_attn_in['bk'], 'L0_attn_Wv': _L0_attn_in['Wv'], 'L0_attn_bv': _L0_attn_in['bv'], 'L0_attn_Wo': _L0_attn_in['Wo'], 'L0_attn_bo': _L0_attn_in['bo'], 'L0_attn_latent_keys': _L0_attn_in['latent_keys'], 'L0_xattn_Wq': _L0_xattn_in['Wq'], 'L0_xattn_w_kc_q': _L0_xattn_in['w_kc_q'], 'L0_xattn_w_kc_kv': _L0_xattn_in['w_kc_kv'], 'L0_xattn_W_qr': _L0_xattn_in['W_qr'], 'L0_xattn_W_kr': _L0_xattn_in['W_kr'], 'L0_xattn_Wo': _L0_xattn_in['Wo'], 'L0_ffn_w1': _L0_ffn_in['w1'], 'L0_ffn_g1': _L0_ffn_in['g1'], 'L0_ffn_w2': _L0_ffn_in['w2'], 'L0_ffn_g2': _L0_ffn_in['g2'], 'L0_ffn_w3': _L0_ffn_in['w3'], 'L0_ffn_g3': _L0_ffn_in['g3']}

def reference(x, ctx_512, L0_attn_Wq, L0_attn_bq, L0_attn_Wk, L0_attn_bk, L0_attn_Wv, L0_attn_bv, L0_attn_Wo, L0_attn_bo, L0_attn_latent_keys, L0_xattn_Wq, L0_xattn_w_kc_q, L0_xattn_w_kc_kv, L0_xattn_W_qr, L0_xattn_W_kr, L0_xattn_Wo, L0_ffn_w1, L0_ffn_g1, L0_ffn_w2, L0_ffn_g2, L0_ffn_w3, L0_ffn_g3):
    import jax
    import jax.numpy as jnp

    def _L0_attn_ref(hidden_states, Wq, bq, Wk, bk, Wv, bv, Wo, bo, latent_keys):
        import jax, jax.numpy as jnp
        import numpy as np
        import math
        B, T, D = (4, 512, 256)
        H = 16
        HD = D // H
        L = 64
        K_TOP = 4
        b, t, d = hidden_states.shape
        Q = (hidden_states @ Wq.T + bq).reshape(b, t, H, HD).transpose(0, 2, 1, 3)
        K = (hidden_states @ Wk.T + bk).reshape(b, t, H, HD).transpose(0, 2, 1, 3)
        V = (hidden_states @ Wv.T + bv).reshape(b, t, H, HD).transpose(0, 2, 1, 3)
        latent = latent_keys.reshape(L, H, HD)
        attn_logits = jnp.einsum('bhtd,lhd->bhtl', Q, latent) / math.sqrt(HD)
        topk_logits, topk_idx = jax.lax.top_k(attn_logits, K_TOP)
        attn_weights = jax.nn.softmax(topk_logits, axis=-1)
        latent_h = latent.transpose(1, 0, 2)
        selected = latent_h[jnp.arange(H)[None, :, None, None], topk_idx]
        weighted = jnp.einsum('bhtk,bhtkd->bhtd', attn_weights, selected)
        attn_output = (weighted + V).transpose(0, 2, 1, 3).reshape(b, t, d)
        return attn_output @ Wo.T + bo

    def _L0_xattn_ref(hidden_q, kv_c, Wq, w_kc_q, w_kc_kv, W_qr, W_kr, Wo):
        import jax, jax.numpy as jnp
        import numpy as np
        B, S, L = (2, 128, 128)
        DIM_Q, H, K, D_C, D_CQ, R = (256, 16, 128, 64, 192, 64)

        def _rope_tables(seq_len, dim, dtype):
            inv_freq = 1.0 / 10000.0 ** (jnp.arange(0, dim, 2, dtype=dtype) / dim)
            t = jnp.arange(seq_len, dtype=dtype)
            freqs = t[:, None] * inv_freq[None, :]
            sin = jnp.repeat(jnp.sin(freqs), 2, axis=-1)
            cos = jnp.repeat(jnp.cos(freqs), 2, axis=-1)
            return (sin, cos)

        def _rotate_half(x):
            h = x.shape[-1] // 2
            return jnp.concatenate([-x[..., h:], x[..., :h]], axis=-1)
        b, s, _ = hidden_q.shape
        l = kv_c.shape[1]
        q_hk = (hidden_q @ Wq.T).reshape(b, s, H, K)
        q_big = jnp.einsum('bshk,hkq->bshq', q_hk, w_kc_q)
        sin, cos = _rope_tables(l, D_C, kv_c.dtype)
        kv_rope = kv_c * cos[None] + _rotate_half(kv_c) * sin[None]
        q_r = jnp.einsum('bshq,hqr->bhsr', q_big, W_qr)
        k_r = jnp.einsum('bld,hdr->bhlr', kv_rope, W_kr)
        scores = jnp.einsum('bhsr,bhlr->bhsl', q_r, k_r)
        attn = jax.nn.softmax(scores, axis=-1)
        ctx_c = jnp.einsum('bhsl,bld->bhsd', attn, kv_rope)
        ctx_lat = jnp.einsum('bhsd,hkd->bshk', ctx_c, w_kc_kv)
        out = ctx_lat.reshape(b, s, H * K) @ Wo.T
        return out

    def _L0_ffn_ref(x, w1, g1, w2, g2, w3, g3):
        import jax, jax.numpy as jnp
        import numpy as np
        EPS = 1e-08

        def _rmsnorm(x, g):
            return g * (x * jax.lax.rsqrt(jnp.mean(x * x, axis=-1, keepdims=True) + EPS))

        def _act_quant(x):
            scale = 127.0 / jnp.clip(jnp.max(jnp.abs(x), axis=-1, keepdims=True), 0.0001, None)
            y = jnp.clip(jnp.round(x * scale), -128, 127) / scale
            return x + jax.lax.stop_gradient(y - x)

        def _ternary_quant(w):
            s = jnp.mean(jnp.abs(w))
            wq = jnp.round(jnp.tanh(w / (s + EPS))) * jnp.arctanh(s)
            return w + jax.lax.stop_gradient(wq - w)

        def _linear_bit(x, w, g):
            xq = _act_quant(_rmsnorm(x, g))
            wq = _ternary_quant(w)
            return jnp.einsum('bsd,od->bso', xq, wq)
        swish = jax.nn.silu(_linear_bit(x, w1, g1))
        x_v = _linear_bit(x, w2, g2)
        h = swish * x_v
        return _linear_bit(h, w3, g3)
    x = _layernorm(x + _L0_attn_ref(x, L0_attn_Wq, L0_attn_bq, L0_attn_Wk, L0_attn_bk, L0_attn_Wv, L0_attn_bv, L0_attn_Wo, L0_attn_bo, L0_attn_latent_keys), axis=-1)
    x = _layernorm(x + _L0_xattn_ref(x, ctx_512, L0_xattn_Wq, L0_xattn_w_kc_q, L0_xattn_w_kc_kv, L0_xattn_W_qr, L0_xattn_W_kr, L0_xattn_Wo), axis=-1)
    x = _layernorm(x + _L0_ffn_ref(x, L0_ffn_w1, L0_ffn_g1, L0_ffn_w2, L0_ffn_g2, L0_ffn_w3, L0_ffn_g3), axis=-1)
    return x

_drawn_inputs = setup_inputs


def setup_inputs(seed=0):
    import zlib

    import numpy as np

    out = dict(_drawn_inputs(seed))
    spreads = {'L0_ffn_g1': (1.0, 0.2), 'L0_ffn_g2': (1.0, 0.2), 'L0_ffn_g3': (1.0, 0.2)}
    factors = {'L0_attn_bq': 10.659}
    for name, (base, spread) in spreads.items():
        noise = np.random.default_rng([zlib.crc32(name.encode()), seed]).standard_normal(out[name].shape)
        drawn = base * np.exp(spread * noise) if base else spread * noise
        out[name] = jnp.asarray(drawn.astype(out[name].dtype))
    for name, factor in factors.items():
        out[name] = (out[name] * factor).astype(out[name].dtype)
    return out
```

```python
from contextlib import ExitStack

import numpy as np

import concourse.bass as bass
from concourse import mybir

ALU = mybir.AluOpType
ACT = mybir.ActivationFunctionType
AX = mybir.AxisListType.X
F32 = mybir.dt.float32
BF16 = mybir.dt.bfloat16

P = 128
D = 256
KD = D // P
BATCH, SEQ = 8, 256
TILES = BATCH * SEQ // P
H = 16
HD = D // H
L = 64
WIDE = H * L
PAIRS = H // 2
TOPK = 4
DC, RR, DCQ, HK = 64, 64, 192, 128
FF = 1024
FC = FF // P
LN_EPS, RMS_EPS, QUANT_MIN = 1e-5, 1e-8, 1e-4
ROUND = 12582912.0
QMAX = 127.0
HALF_ATANH = 0.5493061443340549
ITERS = BATCH + 2
LOOP_FROM, LOOP_TO = 3, 8


def decoder_layer(nc, a, out):
    with ExitStack() as ctx:
        def sb(name, shape, dt=F32):
            return ctx.enter_context(nc.sbuf_tensor(name, shape, dt))

        def sems(*names):
            return [ctx.enter_context(nc.semaphore(n)) for n in names]

        x_sb = sb("x_sb", [P, TILES, D])
        xT = sb("xT", [P, BATCH, KD, SEQ])
        wqT1 = sb("wqT1", [P, KD, D])
        wvT1 = sb("wvT1", [P, KD, D])
        woT1 = sb("woT1", [P, KD, D])
        bqv = sb("bqv", [P, 2, KD])
        bo_row = sb("bo_row", [P, D])
        lat_k = sb("lat_k", [P, KD, 4 * L])
        lat_v = sb("lat_v", [P, PAIRS, 2 * HD])
        ident = sb("ident", [P, P])
        ones = sb("ones", [P, P])
        minus_half = sb("minus_half", [P, 4])
        kv_bd = sb("kv_bd", [P, BATCH, P])
        ctx_raw = sb("ctx_raw", [P, 2, BATCH * L])
        rope_sb = sb("rope_sb", [P, 2, L])
        kv_cur = sb("kv_cur", [P, P])
        A_sb = sb("A_sb", [P, PAIRS, D])
        C_sb = sb("C_sb", [P, PAIRS, D])
        wkrT = sb("wkrT", [RR, H, DC])
        wkckv = sb("wkckv", [P, H, DC])
        T2 = sb("T2", [P, H * DC])
        tern12 = sb("tern12", [P, 2, KD, FF], BF16)
        tern3 = sb("tern3", [P, FC, D], BF16)
        g12 = sb("g12", [P, 2, D])
        g3 = sb("g3", [P, FF])
        region_q = sb("region_q", [P, H * D])
        wqx = region_q[:, :].rearrange("p (h d) -> p h d", h=H)
        w12_raw = region_q[:, :].rearrange("p (w k f) -> p w k f", w=2, k=KD)
        region_c = sb("region_c", [P, 2 * H * HK])
        wkcqT_a = region_c[:, 0:H * HK].rearrange("p (h k) -> p h k", h=H)
        wkcqT_b = region_c[0:DCQ - P, H * HK:2 * H * HK].rearrange("p (h k) -> p h k", h=H)
        w3_raw = region_c[:, 0:FC * D].rearrange("p (c d) -> p c d", c=FC)
        region_o = sb("region_o", [P, H * D])
        woTx = region_o[:, :].rearrange("p (h d) -> p h d", h=H)
        th = region_o[:, 0:FF]
        hh = region_o[:, FF:2 * FF]
        hg = region_o[:, 2 * FF:3 * FF]
        junk_h = region_o[:, 3 * FF:4 * FF]
        region_r = sb("region_r", [P, H * DCQ])
        wqrT = region_r[0:RR, :].rearrange("p (h q) -> p h q", h=H)
        P2 = region_r[:, 0:WIDE]
        PT2 = region_r[:, WIDE:2 * WIDE].rearrange("p (c t) -> p c t", c=PAIRS)
        region_t = sb("region_t", [P, 2 * WIDE])
        T1a, T1b = region_t[:, 0:WIDE], region_t[0:DCQ - P, WIDE:2 * WIDE]
        B_sb = region_t[:, :].rearrange("p (k n) -> p k n", k=KD)
        V_sb = sb("V_sb", [P, PAIRS, D])
        QT = sb("QT", [P, KD, SEQ])
        Ls = sb("Ls", [P, WIDE])
        mask = sb("mask", [P, WIDE])
        m8 = sb("m8", [P, H, 8])
        d4 = sb("d4", [P, H, TOPK])
        r1 = sb("r1", [P, 2, H])
        PT1 = sb("PT1", [P, PAIRS, P])
        AT = sb("AT", [P, KD, P])
        xb = sb("xb", [P, D])
        y = [sb(f"y{k}", [P, D]) for k in (1, 2, 3)]
        x1 = [sb(f"x1_{k}", [P, D]) for k in range(2)]
        x2 = [sb(f"x2_{k}", [P, D]) for k in range(2)]
        x3 = [sb(f"x3_{k}", [P, D]) for k in range(2)]
        x1T = sb("x1T", [P, KD, P])
        m2 = sb("m2", [P, H])
        r2 = sb("r2", [P, 2, H])
        stats = sb("stats", [P, 3, 6])
        moments = sb("moments", [P, 3, 2])
        var3 = sb("var3", [P, 3])
        rstd3 = sb("rstd3", [P, 3])
        xg = sb("xg", [P, 2, D])
        junk_x = sb("junk_x", [P, D])
        sqx = sb("sqx", [P, 4])
        amax = sb("amax", [P, 2])
        cq = sb("cq", [P, 2])
        icq = sb("icq", [P, 2])
        sq = sb("sq", [P, 2])
        dq = sb("dq", [P, 2])
        tq = sb("tq", [P, 2, 2])
        xqT = sb("xqT", [P, 2 * KD, P], BF16)
        sqh = sb("sqh", [P, 4])
        ch = sb("ch", [P, 4])
        dq3 = sb("dq3", [P, 1])
        hqT = sb("hqT", [P, FC, P], BF16)
        atanh_q = sb("atanh_q", [P, 3])
        prep = sb("prep", [P, 10, 3])

        wide = [ctx.enter_context(nc.psum_tensor(f"wide{k}", [P, WIDE], F32)) for k in range(3)]
        small = [ctx.enter_context(nc.psum_tensor(f"small{k}", [P, 512], F32)) for k in range(2)]

        ld_s1, ld_x, ld_ctx, ld_a, ld_c, ld_g, ld_raw, stored = sems(
            "ld_s1", "ld_x", "ld_ctx", "ld_a", "ld_c", "ld_g", "ld_raw", "stored")
        ld_xT = sems(*[f"ld_xT{b}" for b in range(BATCH)])
        c_zero, c_ident, c_const, c_kv, c_chain, c_tern, c_mean = sems(
            "c_zero", "c_ident", "c_const", "c_kv", "c_chain", "c_tern", "c_mean")
        pre_mm, pre_ev, pre_abs, pre_sum, pre_ln, pre_lnin = sems(
            "pre_mm", "pre_ev", "pre_abs", "pre_sum", "pre_ln", "pre_lnin")
        (p_QT, p_x1T, p_xqT, p_L1, p_L2, p_z1, p_z2, p_e0, p_e1, p_PT1, p_WT, p_hT, p_O1, p_PT2,
         p_O2, p_O3) = sems(*("p_QT p_x1T p_xqT p_L1 p_L2 p_z1 p_z2 p_e0 p_e1 p_PT1 p_WT p_hT p_O1 "
                              "p_PT2 p_O2 p_O3").split())
        (a_QT, a_x1T, a_xqT, a_L1, a_e4, a_tanh, a_exp1, a_exp2, a_sqh, a_e0, a_e1, a_sqx, a_PT1,
         a_AT, a_hT, a_PT2) = sems(*("a_QT a_x1T a_xqT a_L1 a_e4 a_tanh a_exp1 a_exp2 a_sqh a_e0 "
                                     "a_e1 a_sqx a_PT1 a_AT a_hT a_PT2").split())
        (v_y1, v_y2, v_y3, v_st1, v_st2, v_st3, v_mom, v_var, v_x1, v_x2, v_x3, v_max8, v_d4,
         v_mask, v_sum1, v_rec1, v_max2, v_sub2, v_sum2, v_rec2, v_u, v_h, v_amax, v_ms, v_cq,
         v_icq, v_sq, v_dq, v_tqh, v_tq, v_quant, v_amaxh, v_msh, v_cqh, v_icqh, v_sqh, v_dqh,
         v_quanth) = sems(*("v_y1 v_y2 v_y3 v_st1 v_st2 v_st3 v_mom v_var v_x1 v_x2 v_x3 v_max8 v_d4 "
                            "v_mask v_sum1 v_rec1 v_max2 v_sub2 v_sum2 v_rec2 v_u v_h v_amax v_ms "
                            "v_cq v_icq v_sq v_dq v_tqh v_tq v_quant v_amaxh v_msh v_cqh v_icqh "
                            "v_sqh v_dqh v_quanth").split())
        (g_rstd, g_xb, g_d1, g_mr, g_P1, g_kv, g_xg, g_rx, g_hg, g_rh, g_P2) = sems(
            *"g_rstd g_xb g_d1 g_mr g_P1 g_kv g_xg g_rx g_hg g_rh g_P2".split())

        def since(eng, sem, count):
            if not isinstance(count, int) or count > 0:
                eng.wait_ge(sem, count)

        def on(n, total=TILES):
            return not isinstance(n, int) or 0 <= n < total

        def spare_done(i, p):
            n = 2 * i + p
            return min(n, 2 * BATCH) if isinstance(n, int) else n

        def heads(ap):
            return ap.rearrange("p (h l) -> p h l", h=H)

        def over_heads(column):
            return column.to_broadcast([P, H, L])

        block = ctx.enter_context(nc.Block())

        @block.sync
        def _(sp):
            sp.dma_start(wqT1[:], a["wqT1"]).then_inc(ld_s1, 16)
            sp.dma_start(xT[:, 0], a["xT"][:, 0]).then_inc(ld_xT[0], 16)
            sp.dma_start(bqv[:], a["bqv"]).then_inc(ld_s1, 16)
            sp.wait_ge(c_zero, 2)
            for q in range(P // HD):
                sp.dma_start(lat_k[HD * q:HD * (q + 1), :, L * (q % 4):L * (q % 4 + 1)],
                             a["latT"][HD * q:HD * (q + 1)]).then_inc(ld_s1, 16)
            for e in range(2):
                sp.dma_start(lat_v[L * e:L * (e + 1), :, HD * e:HD * (e + 1)],
                             a["lat"][:, :, e]).then_inc(ld_s1, 16)
            sp.dma_start(wvT1[:], a["wvT1"]).then_inc(ld_s1, 16)
            sp.dma_start(woT1[:], a["woT1"]).then_inc(ld_s1, 16)
            sp.dma_start(bo_row[:], a["bo"].to_broadcast([P, D])).then_inc(ld_s1, 16)
            sp.dma_start(x_sb[:], a["x"]).then_inc(ld_x, 16)
            sp.dma_start(ctx_raw[:], a["ctxT"]).then_inc(ld_ctx, 16)
            sp.dma_start(rope_sb[:], a["rope"]).then_inc(ld_ctx, 16)
            sp.dma_start(wkrT[:], a["wkrT"]).then_inc(ld_a, 16)
            sp.dma_start(wqrT, a["wqrT"]).then_inc(ld_a, 16)
            sp.dma_start(wkcqT_a, a["wkcqT"][0:P]).then_inc(ld_a, 16)
            sp.dma_start(wkcqT_b, a["wkcqT"][P:DCQ]).then_inc(ld_a, 16)
            sp.dma_start(wqx, a["wqx"]).then_inc(ld_a, 16)
            for b in range(1, BATCH):
                sp.dma_start(xT[:, b], a["xT"][:, b]).then_inc(ld_xT[b], 16)
            sp.dma_start(wkckv[:], a["wkckv"]).then_inc(ld_c, 16)
            sp.dma_start(woTx, a["woTx"]).then_inc(ld_c, 16)
            for k, name in enumerate(("g1", "g2")):
                sp.dma_start(g12[:, k, :], a[name].to_broadcast([P, D])).then_inc(ld_g, 16)
            sp.dma_start(g3[:], a["g3"].to_broadcast([P, FF])).then_inc(ld_g, 16)
            sp.wait_ge(pre_mm, 4)
            sp.dma_start(w12_raw[:, 0], a["w1T"]).then_inc(ld_raw, 16)
            sp.dma_start(w12_raw[:, 1], a["w2T"]).then_inc(ld_raw, 16)
            sp.dma_start(w3_raw, a["w3T"]).then_inc(ld_raw, 16)

            def store(i, p):
                n = 2 * i + p - 5
                if on(n):
                    sp.wait_ge(v_x3, n + 1)
                    sp.dma_start(out[n], x3[1 - p][:]).then_inc(stored, 16)

            for i in range(LOOP_FROM):
                store(i, 0), store(i, 1)
            with sp.Fori(LOOP_FROM, LOOP_TO) as i:
                store(i, 0), store(i, 1)
            for i in range(LOOP_TO, ITERS + 1):
                store(i, 0), store(i, 1)
            sp.wait_ge(stored, 16 * TILES)

        @block.tensor
        def _(pe):
            def slot(i, p):
                t = 2 * i + p
                n1, n2, n3 = t, t - 2, t - 4
                if on(n2):
                    pe.wait_ge(v_x1, n2 + 1)
                    since(pe, v_y2, n2)
                    for k in range(KD):
                        mm = pe.transpose(small[1][:, k * P:(k + 1) * P],
                                          x1[p][:, k * P:(k + 1) * P], ident[:])
                    mm.then_inc(p_x1T, 1)
                if p == 0 and on(i, BATCH):
                    if isinstance(i, int):
                        pe.wait_ge(ld_xT[i], 16)
                    since(pe, v_y3, n3)
                    since(pe, v_y1, n1)
                    for g in range(KD):
                        for k in range(KD):
                            mm = pe.matmul(small[0][:, g * SEQ:(g + 1) * SEQ],
                                           wqT1[:, k, g * P:(g + 1) * P], xT[:, i, k, :],
                                           start=(k == 0), stop=(k == KD - 1))
                    mm.then_inc(p_QT, 1)
                if on(n1):
                    if p == 0:
                        pe.wait_ge(a_QT, i + 1)
                    since(pe, a_PT1, n1)
                    for g in range(KD):
                        for j in range(2):
                            mm = pe.matmul(wide[0][:, j * 512 + g * SEQ:j * 512 + (g + 1) * SEQ],
                                           QT[j * L:(j + 1) * L, g, p * P:(p + 1) * P],
                                           lat_k[j * L:(j + 1) * L, g, :], start=True, stop=True)
                    mm.then_inc(p_L1, 1)
                if on(n3):
                    pe.wait_ge(v_quant, n3 + 1)
                    if p == 0 and on(i, BATCH):
                        pe.wait_ge(a_QT, i + 1)
                    else:
                        since(pe, v_y3, n3)
                        since(pe, v_y1, min(n1, TILES) if isinstance(n1, int) else n1)
                    for k in range(2 * KD):
                        mm = pe.transpose(small[0][:, k * P:(k + 1) * P],
                                          xg[:, k // KD, (k % KD) * P:(k % KD + 1) * P], ident[:])
                    mm.then_inc(p_xqT, 1)
                if on(n2):
                    pe.wait_ge(a_x1T, n2 + 1)
                    since(pe, a_hT, n3)
                    for q in range(2):
                        for k in range(KD):
                            mm = pe.matmul(wide[1][:, q * 512:(q + 1) * 512], x1T[:, k, :],
                                           B_sb[:, k, q * 512:(q + 1) * 512],
                                           start=(k == 0), stop=(k == KD - 1))
                    mm.then_inc(p_L2, 1)
                if on(n3):
                    if isinstance(n3, int) and n3 == 0:
                        pe.wait_ge(c_tern, 3)
                    pe.wait_ge(a_xqT, n3 + 1)
                    since(pe, a_PT2, min(n2, TILES) if isinstance(n2, int) else n2)
                    if on(n1):
                        pe.wait_ge(a_L1, n1 + 1)
                    else:
                        pe.wait_ge(a_PT1, TILES)
                    for w, sem in enumerate((p_z1, p_z2)):
                        for q in range(2):
                            for k in range(KD):
                                mm = pe.matmul(wide[2 - 2 * w][:, q * 512:(q + 1) * 512],
                                               xqT[:, w * KD + k, :],
                                               tern12[:, w, k, q * 512:(q + 1) * 512],
                                               start=(k == 0), stop=(k == KD - 1))
                        mm.then_inc(sem, 1)
                if p == 0 and on(i - 1, BATCH):
                    pe.wait_ge(g_kv, i)
                    pe.wait_ge(v_sub2, n2 + 1)
                    since(pe, v_u, n3 + 1)
                    for half, sem in enumerate((p_e0, p_e1)):
                        for c in range(PAIRS // 2):
                            mm = pe.matmul(wide[1 + half][:, c * D:(c + 1) * D], kv_cur[:],
                                           C_sb[:, half * PAIRS // 2 + c, :], start=True, stop=True)
                        mm.then_inc(sem, 1)
                if p == 1 and on(i, BATCH):
                    if isinstance(i, int) and i == 0:
                        pe.wait_ge(c_kv, 1)
                        pe.wait_ge(pre_ev, 7)
                    since(pe, v_sub2, n2 + 1)
                    since(pe, v_u, n3 + 1)
                    for k, sem in enumerate((p_e0, p_e1)):
                        for c in range(PAIRS):
                            mm = pe.matmul(wide[1 + k][:, c * P:(c + 1) * P],
                                           A_sb[:, c, k * P:(k + 1) * P], kv_bd[:, i, :],
                                           start=True, stop=True)
                        mm.then_inc(sem, 1)
                if on(n1):
                    if on(n2):
                        pe.wait_ge(a_x1T, n2 + 1)
                    for g in range(KD):
                        for k in range(KD):
                            pe.matmul(small[1][:, g * P:(g + 1) * P], wvT1[:, k, g * P:(g + 1) * P],
                                      xT[:, i, k, p * P:(p + 1) * P],
                                      start=(g == 0 and k == 0), stop=False, skip_group_check=True)
                    pe.wait_ge(g_P1, n1 + 1)
                    pe.wait_ge(a_L1, n1 + 1)
                    since(pe, v_h, n3 + 1)
                    for c in range(PAIRS):
                        mm = pe.transpose(wide[0][:, c * P:(c + 1) * P], Ls[:, c * P:(c + 1) * P],
                                          ident[:])
                    mm.then_inc(p_PT1, 1)
                    pe.wait_ge(a_PT1, n1 + 1)
                    for c in range(PAIRS):
                        g, q = divmod(c, PAIRS // KD)
                        mm = pe.matmul(small[1][32 * q:32 * (q + 1), g * P:(g + 1) * P],
                                       lat_v[:, c, :], PT1[:, c, :],
                                       start=False, stop=(c == PAIRS - 1), skip_group_check=True)
                    mm.then_inc(p_WT, 1)
                if on(n3):
                    pe.wait_ge(v_quanth, n3 + 1)
                    since(pe, a_e0, spare_done(i, p))
                    if on(n2):
                        pe.wait_ge(v_sub2, n2 + 1)
                    for c in range(FC):
                        mm = pe.transpose(wide[1][:, c * P:(c + 1) * P], hg[:, c * P:(c + 1) * P],
                                          ident[:])
                    mm.then_inc(p_hT, 1)
                if on(n1):
                    pe.wait_ge(a_AT, n1 + 1)
                    if on(n3):
                        pe.wait_ge(a_xqT, n3 + 1)
                    else:
                        pe.wait_ge(a_QT, i + 1)
                        since(pe, v_y1, n1)
                    for g in range(KD):
                        mm = pe.matmul(small[0][:, 0:D], AT[:, g, :], woT1[:, g, :],
                                       start=(g == 0), stop=(g == KD - 1))
                    mm.then_inc(p_O1, 1)
                if on(n2):
                    pe.wait_ge(g_P2, n2 + 1)
                    since(pe, a_e1, spare_done(i, p))
                    if on(n3):
                        pe.wait_ge(v_u, n3 + 1)
                    for c in range(PAIRS):
                        mm = pe.transpose(wide[2][:, c * P:(c + 1) * P], P2[:, c * P:(c + 1) * P],
                                          ident[:])
                    mm.then_inc(p_PT2, 1)
                    pe.wait_ge(a_PT2, n2 + 1)
                    if on(n1):
                        pe.wait_ge(a_AT, n1 + 1)
                    for c in range(PAIRS):
                        mm = pe.matmul(small[1][:, 0:D], PT2[:, c, :], V_sb[:, c, :],
                                       start=(c == 0), stop=(c == PAIRS - 1))
                    mm.then_inc(p_O2, 1)
                if on(n3):
                    pe.wait_ge(a_hT, n3 + 1)
                    if on(n1):
                        pe.wait_ge(v_y1, n1 + 1)
                    for c in range(FC):
                        mm = pe.matmul(small[0][:, 0:D], hqT[:, c, :], tern3[:, c, :],
                                       start=(c == 0), stop=(c == FC - 1))
                    mm.then_inc(p_O3, 1)

            def cross_weights():
                pe.wait_ge(ld_a, 16 * 5)
                for half, (lo, hi) in enumerate(((0, P), (P, DCQ))):
                    for h in range(H):
                        mm = pe.matmul(wide[1 + half][0:hi - lo, h * DC:(h + 1) * DC],
                                       wqrT[:, h, lo:hi], wkrT[:, h, :], start=True, stop=True)
                    mm.then_inc(pre_mm, 1)
                pe.wait_ge(pre_ev, 2)
                for h in range(H):
                    pe.matmul(wide[0][:, h * DC:(h + 1) * DC], wkcqT_a[:, h, :],
                              T1a[:, h * DC:(h + 1) * DC], start=True, stop=False)
                    mm = pe.matmul(wide[0][:, h * DC:(h + 1) * DC], wkcqT_b[:, h, :],
                                   T1b[:, h * DC:(h + 1) * DC], start=False, stop=True)
                mm.then_inc(pre_mm, 1)
                pe.wait_ge(pre_ev, 3)
                for h in range(H):
                    c, e = divmod(h, 2)
                    mm = pe.matmul(wide[1 + c // 4][DC * e:DC * (e + 1), (c % 4) * D:(c % 4 + 1) * D],
                                   T2[:, h * DC:(h + 1) * DC], wqx[:, h, :], start=True, stop=True)
                mm.then_inc(pre_mm, 1)
                pe.wait_ge(ld_c, 16 * 2)
                for half in range(2):
                    pe.wait_ge(pre_ev, 3 + half)
                    for h in range(half * H // 2, (half + 1) * H // 2):
                        c, e = divmod(h, 2)
                        mm = pe.matmul(wide[half][DC * e:DC * (e + 1), (c % 4) * D:(c % 4 + 1) * D],
                                       wkckv[:, h, :], woTx[:, h, :], start=True, stop=True)
                    mm.then_inc(pre_mm, 1)
                pe.wait_ge(pre_ev, 7)

            def ffn_sums():
                pe.wait_ge(pre_abs, 3)
                pe.wait_ge(v_y1, 3)
                pe.matmul(small[0][:, 0:3], ones[:], prep[:, 0, :], start=True, stop=True
                          ).then_inc(pre_sum, 1)

            pe.wait_ge(ld_s1, 16 * 15)
            pe.wait_ge(c_ident, 1)
            slot(0, 0)
            cross_weights()
            slot(0, 1)
            slot(1, 0)
            ffn_sums()
            pe.wait_ge(c_mean, 1)
            slot(1, 1)
            for i in range(2, LOOP_FROM):
                slot(i, 0), slot(i, 1)
            for b in range(LOOP_FROM, BATCH):
                pe.wait_ge(ld_xT[b], 16)
            with pe.Fori(LOOP_FROM, LOOP_TO) as i:
                slot(i, 0), slot(i, 1)
            for i in range(LOOP_TO, ITERS):
                slot(i, 0), slot(i, 1)

        @block.scalar
        def _(act):
            def slot(i, p):
                t = 2 * i + p
                n1, n2, n3, nf = t, t - 2, t - 4, t - 3
                if on(n2):
                    act.wait_ge(p_x1T, n2 + 1)
                    since(act, p_L2, n2)
                    act.activation(x1T[:], small[1][:, 0:D].rearrange("p (k t) -> p k t", k=KD),
                                   ACT.Copy).then_inc(a_x1T, 1)
                if p == 0 and on(i, BATCH):
                    act.wait_ge(p_QT, i + 1)
                    since(act, p_L1, n1)
                    for g in range(KD):
                        ins = act.activation(QT[:, g, :], small[0][:, g * SEQ:(g + 1) * SEQ],
                                             ACT.Identity, bias=bqv[:, 0, g:g + 1])
                    ins.then_inc(a_QT, 1)
                if on(n1):
                    act.wait_ge(p_L1, n1 + 1)
                    since(act, p_PT1, n1)
                    for j in range(2):
                        ins = act.activation(
                            Ls[:].rearrange("p (g j n) -> p j g n", g=KD, j=2)[:, j],
                            wide[0][:, j * 512:(j + 1) * 512].rearrange("p (g n) -> p g n", g=KD),
                            ACT.Copy)
                    ins.then_inc(a_L1, 1)
                if on(n3):
                    act.wait_ge(p_xqT, n3 + 1)
                    since(act, p_z2, n3)
                    act.activation(xqT[:], small[0][:].rearrange("p (k t) -> p k t", k=2 * KD),
                                   ACT.Copy, bias=-ROUND).then_inc(a_xqT, 1)
                if on(n1):
                    act.wait_ge(v_d4, n1 + 1)
                    act.activation(d4[:], d4[:], ACT.Exp, scale=HD ** -0.5).then_inc(a_e4, 1)
                if on(n3):
                    act.wait_ge(p_z1, n3 + 1)
                    act.wait_ge(v_tq, n3 + 1)
                    since(act, v_h, n3)
                    act.activation(th, wide[2][:], ACT.Tanh, scale=tq[:, p, 0:1]).then_inc(a_tanh, 1)
                if on(n1):
                    act.wait_ge(g_d1, n1 + 1)
                    act.activation(Ls[:], Ls[:], ACT.Exp, scale=HD ** -0.5).then_inc(a_exp1, 1)
                if on(n2):
                    act.wait_ge(v_sub2, n2 + 1)
                    act.activation(P2, P2, ACT.Exp).then_inc(a_exp2, 1)
                if on(nf):
                    act.wait_ge(v_x2, nf + 1)
                    since(act, a_sqx, nf)
                    act.activation(junk_x[:], x2[1 - p][:], ACT.Square,
                                   accum_out=sqx[:, 0:1]).then_inc(a_sqx, 1)
                if on(n3):
                    act.wait_ge(v_h, n3 + 1)
                    since(act, a_sqh, n3)
                    act.activation(junk_h, hh, ACT.Square, accum_out=sqh[:, 0:1]).then_inc(a_sqh, 1)
                for half, (ready, copied) in enumerate(((p_e0, a_e0), (p_e1, a_e1))):
                    if p == 0 and on(i - 1, BATCH):
                        act.wait_ge(ready, spare_done(i, p))
                        since(act, p_O2, n2)
                        act.activation(V_sb[:, half * 4:(half + 1) * 4, :],
                                       wide[1 + half][:].rearrange("p (c n) -> p c n", c=4),
                                       ACT.Copy).then_inc(copied, 1)
                    if p == 1 and on(i, BATCH):
                        act.wait_ge(ready, spare_done(i, p))
                        act.activation(B_sb[:, half, :], wide[1 + half][:], ACT.Copy
                                       ).then_inc(copied, 1)
                if on(n1):
                    act.wait_ge(p_PT1, n1 + 1)
                    since(act, p_WT, n1)
                    act.activation(PT1[:], wide[0][:].rearrange("p (c t) -> p c t", c=PAIRS),
                                   ACT.Copy).then_inc(a_PT1, 1)
                    act.wait_ge(p_WT, n1 + 1)
                    since(act, p_O1, n1)
                    for g in range(KD):
                        ins = act.activation(AT[:, g, :], small[1][:, g * P:(g + 1) * P],
                                             ACT.Identity, bias=bqv[:, 1, g:g + 1])
                    ins.then_inc(a_AT, 1)
                if on(n3):
                    act.wait_ge(p_hT, n3 + 1)
                    since(act, p_O3, n3)
                    act.activation(hqT[:], wide[1][:].rearrange("p (c t) -> p c t", c=FC),
                                   ACT.Copy, bias=-ROUND).then_inc(a_hT, 1)
                if on(n2):
                    act.wait_ge(p_PT2, n2 + 1)
                    since(act, p_O2, n2)
                    act.activation(PT2, wide[2][:].rearrange("p (c t) -> p c t", c=PAIRS),
                                   ACT.Copy).then_inc(a_PT2, 1)

            def cross_weights():
                act.wait_ge(pre_mm, 1)
                act.activation(T1a, wide[1][:], ACT.Copy).then_inc(pre_ev, 1)
                act.wait_ge(pre_mm, 2)
                act.activation(T1b, wide[2][0:DCQ - P, :], ACT.Copy).then_inc(pre_ev, 1)
                act.wait_ge(pre_mm, 3)
                act.activation(T2[:], wide[0][:], ACT.Copy).then_inc(pre_ev, 1)
                act.wait_ge(pre_mm, 4)
                for half in range(2):
                    act.activation(A_sb[:, 4 * half:4 * half + 4, :],
                                   wide[1 + half][:].rearrange("p (c n) -> p c n", c=4),
                                   ACT.Copy).then_inc(pre_ev, 1)
                for half in range(2):
                    act.wait_ge(pre_mm, 5 + half)
                    act.activation(C_sb[:, 4 * half:4 * half + 4, :],
                                   wide[half][:].rearrange("p (c n) -> p c n", c=4),
                                   ACT.Copy).then_inc(pre_ev, 1)

            def ffn_sums():
                act.wait_ge(ld_raw, 16 * 3)
                for w in range(2):
                    act.activation(tern12[:, w].rearrange("p k f -> p (k f)"),
                                   w12_raw[:, w].rearrange("p k f -> p (k f)"), ACT.Abs,
                                   accum_out=prep[:, 0, w:w + 1]).then_inc(pre_abs, 1)
                act.activation(tern3[:].rearrange("p c d -> p (c d)"),
                               w3_raw.rearrange("p c d -> p (c d)"), ACT.Abs,
                               accum_out=prep[:, 0, 2:3]).then_inc(pre_abs, 1)
                act.wait_ge(pre_lnin, 1)
                act.activation(prep[:, 5, :], prep[:, 4, :], ACT.Ln).then_inc(pre_ln, 1)

            act.wait_ge(ld_s1, 16 * 15)
            slot(0, 0)
            cross_weights()
            slot(0, 1)
            slot(1, 0)
            ffn_sums()
            slot(1, 1)
            for i in range(2, LOOP_FROM):
                slot(i, 0), slot(i, 1)
            with act.Fori(LOOP_FROM, LOOP_TO) as i:
                slot(i, 0), slot(i, 1)
            for i in range(LOOP_TO, ITERS):
                slot(i, 0), slot(i, 1)

        @block.vector
        def _(dve):
            def moments_of(k, n, sem_y, sem_st):
                dve.wait_ge(sem_y, n + 1)
                dve.bn_stats(stats[:, k, :], y[k][:]).then_inc(sem_st, 1)
                dve.wait_ge(c_zero, 3)
                dve.wait_ge(sem_st, n + 1)
                dve.bn_aggr(moments[:, k, :], stats[:, k, :]).then_inc(v_mom, 1)

            def slot(i, p):
                t = 2 * i + p
                n1, n2, n3, nf = t, t - 2, t - 4, t - 3
                e1, e2, e3, q = t - 1, t - 3, t - 5, 1 - p

                def moments_done():
                    if not isinstance(t, int):
                        return 3 * t - 6
                    return sum(max(0, min(n + 1, TILES)) for n in (e1, e2, e3))

                if on(e2):
                    dve.wait_ge(p_O2, e2 + 1)
                    since(dve, v_x2, e2)
                    dve.tensor_tensor(y[1][:], small[1][:, 0:D], x1[q][:], ALU.add).then_inc(v_y2, 1)
                if on(e3):
                    dve.wait_ge(p_O3, e3 + 1)
                    dve.wait_ge(v_dqh, e3 + 1)
                    since(dve, v_x3, e3)
                    dve.scalar_tensor_tensor(y[2][:], small[0][:, 0:D], dq3[:, 0:1], x2[q][:],
                                             ALU.mult, ALU.add).then_inc(v_y3, 1)
                if on(e2):
                    moments_of(1, e2, v_y2, v_st2)
                if on(e3):
                    moments_of(2, e3, v_y3, v_st3)
                if on(n1):
                    dve.wait_ge(a_L1, n1 + 1)
                    since(dve, g_d1, n1)
                if on(e1) or on(e2) or on(e3):
                    dve.wait_ge(v_mom, moments_done())
                    dve.tensor_scalar(var3[:], moments[:, :, 1], LN_EPS, None, ALU.add
                                      ).then_inc(v_var, 1)
                if on(n1):
                    for h in range(H):
                        ins = dve.max(m8[:, h, :], Ls[:, h * L:(h + 1) * L])
                    ins.then_inc(v_max8, 1)
                    dve.wait_ge(v_max8, n1 + 1)
                    dve.tensor_tensor(d4[:], m8[:, :, 0:TOPK],
                                      m8[:, :, 0:1].to_broadcast([P, H, TOPK]), ALU.subtract
                                      ).then_inc(v_d4, 1)
                    since(dve, g_P1, n1)
                    dve.tensor_tensor(heads(mask[:]), heads(Ls[:]),
                                      over_heads(m8[:, :, TOPK - 1:TOPK]), ALU.is_ge
                                      ).then_inc(v_mask, 1)
                    dve.wait_ge(a_e4, n1 + 1)
                    dve.tensor_reduce(r1[:, 0, :], d4[:], AX, ALU.add).then_inc(v_sum1, 1)
                    dve.wait_ge(v_sum1, n1 + 1)
                    since(dve, g_mr, n1)
                    dve.reciprocal(r1[:, 1, :], r1[:, 0, :]).then_inc(v_rec1, 1)
                if on(n2):
                    dve.wait_ge(p_L2, n2 + 1)
                    dve.tensor_reduce(m2[:], heads(wide[1][:]), AX, ALU.max).then_inc(v_max2, 1)
                    dve.wait_ge(v_max2, n2 + 1)
                    since(dve, p_PT2, n2)
                    dve.tensor_tensor(heads(P2), heads(wide[1][:]),
                                      over_heads(m2[:].rearrange("p (h o) -> p h o", o=1)),
                                      ALU.subtract).then_inc(v_sub2, 1)
                if on(e1) or on(e2) or on(e3):
                    dve.wait_ge(g_rstd, t)
                for k, (n, dst, sem) in enumerate(((e1, x1, v_x1), (e2, x2, v_x2), (e3, x3, v_x3))):
                    if on(n):
                        if k == 0:
                            since(dve, p_x1T, n - 1)
                        if k == 2:
                            since(dve, stored, 16 * n)
                        dve.tensor_scalar(dst[q][:], y[k][:], moments[:, k, 0:1], rstd3[:, k:k + 1],
                                          ALU.subtract, ALU.mult).then_inc(sem, 1)
                if on(n3):
                    dve.wait_ge(a_tanh, n3 + 1)
                    dve.scalar_tensor_tensor(th, th, 1.0, wide[2][:], ALU.add, ALU.mult
                                             ).then_inc(v_u, 1)
                    dve.wait_ge(v_u, n3 + 1)
                    dve.wait_ge(p_z2, n3 + 1)
                    since(dve, a_sqh, n3)
                    since(dve, g_hg, n3)
                    dve.scalar_tensor_tensor(hh, wide[0][:], tq[:, p, 1:2], th, ALU.mult, ALU.mult
                                             ).then_inc(v_h, 1)
                if on(n2):
                    dve.wait_ge(a_exp2, n2 + 1)
                    dve.tensor_reduce(r2[:, 0, :], heads(P2), AX, ALU.add).then_inc(v_sum2, 1)
                    dve.wait_ge(v_sum2, n2 + 1)
                    dve.reciprocal(r2[:, 1, :], r2[:, 0, :]).then_inc(v_rec2, 1)
                if on(nf):
                    dve.wait_ge(a_sqx, nf + 1)
                    dve.tensor_scalar(sqx[:, 1:2], sqx[:, 0:1], 1.0 / D, RMS_EPS, ALU.mult, ALU.add
                                      ).then_inc(v_ms, 1)
                    dve.wait_ge(g_xg, nf + 1)
                    dve.tensor_reduce(amax[:], xg[:], AX, ALU.max, apply_absolute_value=True
                                      ).then_inc(v_amax, 1)
                    dve.wait_ge(v_amax, nf + 1)
                    dve.wait_ge(g_rx, nf + 1)
                    dve.tensor_scalar(cq[:], amax[:], sqx[:, 2:3], QUANT_MIN, ALU.mult, ALU.max
                                      ).then_inc(v_cq, 1)
                    dve.wait_ge(v_cq, nf + 1)
                    dve.reciprocal(icq[:], cq[:]).then_inc(v_icq, 1)
                    dve.tensor_tensor(dq[:], cq[:], atanh_q[:, 0:2], ALU.mult).then_inc(v_dq, 1)
                    dve.wait_ge(v_icq, nf + 1)
                    dve.tensor_scalar(sq[:], icq[:], sqx[:, 2:3], QMAX, ALU.mult, ALU.mult
                                      ).then_inc(v_sq, 1)
                    dve.wait_ge(v_dq, nf + 1)
                    dve.tensor_scalar(tq[:, q, 0:1], dq[:, 0:1], 0.5, None, ALU.mult
                                      ).then_inc(v_tqh, 1)
                    dve.wait_ge(v_tqh, nf + 1)
                    dve.tensor_tensor(tq[:, q, 1:2], tq[:, q, 0:1], dq[:, 1:2], ALU.mult
                                      ).then_inc(v_tq, 1)
                    dve.wait_ge(v_sq, nf + 1)
                    for k in range(2):
                        ins = dve.tensor_scalar(xg[:, k, :], xg[:, k, :], sq[:, k:k + 1], ROUND,
                                                ALU.mult, ALU.add)
                    ins.then_inc(v_quant, 1)
                if on(n3):
                    dve.wait_ge(a_sqh, n3 + 1)
                    dve.tensor_scalar(sqh[:, 1:2], sqh[:, 0:1], 1.0 / FF, RMS_EPS, ALU.mult, ALU.add
                                      ).then_inc(v_msh, 1)
                    dve.wait_ge(g_hg, n3 + 1)
                    dve.tensor_reduce(ch[:, 0:1], hg, AX, ALU.max, apply_absolute_value=True
                                      ).then_inc(v_amaxh, 1)
                    dve.wait_ge(v_amaxh, n3 + 1)
                    dve.wait_ge(g_rh, n3 + 1)
                    dve.tensor_scalar(ch[:, 1:2], ch[:, 0:1], sqh[:, 2:3], QUANT_MIN, ALU.mult,
                                      ALU.max).then_inc(v_cqh, 1)
                    dve.wait_ge(v_cqh, n3 + 1)
                    dve.reciprocal(ch[:, 2:3], ch[:, 1:2]).then_inc(v_icqh, 1)
                    dve.tensor_tensor(dq3[:], ch[:, 1:2], atanh_q[:, 2:3], ALU.mult
                                      ).then_inc(v_dqh, 1)
                    dve.wait_ge(v_icqh, n3 + 1)
                    dve.tensor_scalar(ch[:, 3:4], ch[:, 2:3], sqh[:, 2:3], QMAX, ALU.mult, ALU.mult
                                      ).then_inc(v_sqh, 1)
                    dve.wait_ge(v_sqh, n3 + 1)
                    dve.tensor_scalar(hg, hg, ch[:, 3:4], ROUND, ALU.mult, ALU.add
                                      ).then_inc(v_quanth, 1)
                if on(n1):
                    dve.wait_ge(p_O1, n1 + 1)
                    dve.wait_ge(g_xb, n1 + 1)
                    since(dve, v_x1, n1)
                    dve.tensor_tensor(y[0][:], small[0][:, 0:D], xb[:], ALU.add).then_inc(v_y1, 1)
                    moments_of(0, n1, v_y1, v_st1)

            chain = [0]

            def link(ins):
                chain[0] += 1
                ins.then_inc(c_chain, 1)
                dve.wait_ge(c_chain, chain[0])

            def atanh_weights():
                dve.wait_ge(pre_sum, 1)
                mean, one_m, ratio, ln_in, ln_out = (prep[:, k, :] for k in (1, 2, 3, 4, 5))
                sq_, acc, small_s, low = (prep[:, k, :] for k in (6, 7, 8, 9))
                dve.tensor_scalar(mean, small[0][:, 0:3], 1.0 / (D * FF), None, ALU.mult
                                  ).then_inc(c_mean, 1)
                dve.wait_ge(c_mean, 1)
                link(dve.tensor_scalar(one_m, mean, -1.0, 1.0, ALU.mult, ALU.add))
                link(dve.reciprocal(ratio, one_m))
                link(dve.scalar_tensor_tensor(ln_in, mean, 1.0, ratio, ALU.add, ALU.mult))
                dve.tensor_tensor(sq_, mean, mean, ALU.mult).then_inc(pre_lnin, 1)
                dve.wait_ge(pre_lnin, 1)
                link(dve.tensor_scalar(acc, sq_, 1.0 / 17.0, None, ALU.mult))
                for k in (15, 13, 11, 9, 7, 5, 3):
                    link(dve.scalar_tensor_tensor(acc, acc, 1.0 / k, sq_, ALU.add, ALU.mult))
                link(dve.scalar_tensor_tensor(acc, acc, 1.0, mean, ALU.add, ALU.mult))
                link(dve.tensor_scalar(low, mean, 0.25, None, ALU.is_lt))
                dve.wait_ge(pre_ln, 1)
                link(dve.tensor_scalar(small_s, ln_out, 0.5, None, ALU.mult))
                link(dve.tensor_tensor(acc, acc, small_s, ALU.subtract))
                link(dve.tensor_tensor(acc, acc, low, ALU.mult))
                link(dve.tensor_tensor(acc, acc, small_s, ALU.add))
                link(dve.tensor_scalar(atanh_q[:], acc, 1.0 / QMAX, None, ALU.mult))
                link(dve.tensor_scalar(small_s, mean, RMS_EPS, HALF_ATANH, ALU.add, ALU.mult))
                link(dve.tensor_scalar(low, small_s, -1.0, None, ALU.mult))

            def ternary_weights():
                for w, (raw, dst) in enumerate(((w12_raw[:, 0], tern12[:, 0]),
                                                (w12_raw[:, 1], tern12[:, 1]), (w3_raw, tern3[:]))):
                    raw, dst = (v.rearrange("p a b -> p (a b)") for v in (raw, dst))
                    link(dve.tensor_scalar(dst, raw, prep[:, 9, w:w + 1], None, ALU.is_lt))
                    dve.scalar_tensor_tensor(dst, raw, prep[:, 8, w:w + 1], dst, ALU.is_gt,
                                             ALU.subtract).then_inc(c_tern, 1)

            def rope():
                dve.wait_ge(ld_ctx, 16 * 2)
                ctx3 = [ctx_raw[:, r, :].rearrange("p (b l) -> p b l", b=BATCH) for r in range(2)]
                for r in range(2):
                    table = rope_sb[:, r:r + 1, :].to_broadcast([P, BATCH, L])
                    link(dve.tensor_tensor(ctx3[r], ctx3[r], table, ALU.mult))
                dve.wait_ge(c_zero, 3)
                for e in range(2):
                    r = slice(e * L, (e + 1) * L)
                    ins = dve.tensor_tensor(kv_bd[r, :, e * L:(e + 1) * L], ctx3[0][r], ctx3[1][r],
                                            ALU.add)
                ins.then_inc(c_kv, 1)

            link(dve.memset(moments[:], 1.0))
            dve.wait_ge(ld_s1, 16 * 15)
            slot(0, 0)
            rope()
            slot(0, 1)
            slot(1, 0)
            atanh_weights()
            slot(1, 1)
            ternary_weights()
            for i in range(2, LOOP_FROM):
                slot(i, 0), slot(i, 1)
            with dve.Fori(LOOP_FROM, LOOP_TO) as i:
                slot(i, 0), slot(i, 1)
            for i in range(LOOP_TO, ITERS):
                slot(i, 0), slot(i, 1)
            slot(ITERS, 0)

        @block.gpsimd
        def _(pool):
            def slot(i, p):
                t = 2 * i + p
                n1, n2, n3, nf = t, t - 2, t - 4, t - 3
                e1, e2, e3, q = t - 1, t - 3, t - 5, 1 - p
                if on(e1) or on(e2) or on(e3):
                    pool.wait_ge(v_var, t)
                    pool.tensor_tensor(rstd3[:], var3[:], minus_half[:, 0:3], ALU.pow
                                       ).then_inc(g_rstd, 1)
                if p == 0 and on(i - 1, BATCH):
                    since(pool, p_e1, spare_done(i - 1, 0))
                    pool.tensor_copy(kv_cur[:], kv_bd[:, i - 1, :]).then_inc(g_kv, 1)
                if on(n1):
                    since(pool, v_y1, n1)
                    pool.tensor_tensor(xb[:], x_sb[:, n1, :], bo_row[:], ALU.add).then_inc(g_xb, 1)
                    pool.wait_ge(v_mask, n1 + 1)
                    pool.tensor_tensor(heads(Ls[:]), heads(Ls[:]), over_heads(m8[:, :, 0:1]),
                                       ALU.subtract).then_inc(g_d1, 1)
                    pool.wait_ge(v_rec1, n1 + 1)
                    pool.tensor_tensor(heads(mask[:]), heads(mask[:]),
                                       over_heads(r1[:, 1, :].rearrange("p (h o) -> p h o", o=1)),
                                       ALU.mult).then_inc(g_mr, 1)
                    pool.wait_ge(g_mr, n1 + 1)
                    pool.wait_ge(a_exp1, n1 + 1)
                    pool.tensor_tensor(Ls[:], Ls[:], mask[:], ALU.mult).then_inc(g_P1, 1)
                if on(nf):
                    pool.wait_ge(v_x2, nf + 1)
                    since(pool, p_xqT, nf)
                    pool.tensor_tensor(xg[:], x2[q][:].rearrange("p (o d) -> p o d", o=1)
                                       .to_broadcast([P, 2, D]), g12[:], ALU.mult).then_inc(g_xg, 1)
                    pool.wait_ge(v_ms, nf + 1)
                    pool.tensor_tensor(sqx[:, 2:3], sqx[:, 1:2], minus_half[:, 0:1], ALU.pow
                                       ).then_inc(g_rx, 1)
                if on(n3):
                    pool.wait_ge(v_h, n3 + 1)
                    since(pool, p_hT, n3)
                    pool.tensor_tensor(hg, hh, g3[:], ALU.mult).then_inc(g_hg, 1)
                    pool.wait_ge(v_msh, n3 + 1)
                    pool.tensor_tensor(sqh[:, 2:3], sqh[:, 1:2], minus_half[:, 0:1], ALU.pow
                                       ).then_inc(g_rh, 1)
                if on(n2):
                    pool.wait_ge(v_rec2, n2 + 1)
                    pool.tensor_tensor(heads(P2), heads(P2),
                                       over_heads(r2[:, 1, :].rearrange("p (h o) -> p h o", o=1)),
                                       ALU.mult).then_inc(g_P2, 1)

            pool.memset(lat_k[:], 0.0).then_inc(c_zero, 1)
            pool.memset(lat_v[:], 0.0).then_inc(c_zero, 1)
            pool.memset(kv_bd[:], 0.0).then_inc(c_zero, 1)
            pool.memset(ident[:], 0.0).then_inc(c_const, 1)
            pool.memset(ones[:], 1.0).then_inc(c_const, 1)
            pool.memset(minus_half[:], -0.5).then_inc(c_const, 1)
            pool.wait_ge(c_const, 3)
            pool.affine_select(out=ident[:], in_=ident[:], compare_op=ALU.not_equal, fill=1.0,
                               base=0, pattern=[[-1, P]], channel_multiplier=1).then_inc(c_ident, 1)
            pool.wait_ge(ld_x, 16)
            pool.wait_ge(ld_s1, 16 * 15)
            slot(0, 0)
            slot(0, 1)
            pool.wait_ge(c_kv, 1)
            slot(1, 0)
            pool.wait_ge(ld_g, 16 * 3)
            slot(1, 1)
            for i in range(2, LOOP_FROM):
                slot(i, 0), slot(i, 1)
            with pool.Fori(LOOP_FROM, LOOP_TO) as i:
                slot(i, 0), slot(i, 1)
            for i in range(LOOP_TO, ITERS):
                slot(i, 0), slot(i, 1)
            slot(ITERS, 0)


def rope_tables():
    inv_freq = (1.0 / (10000.0 ** (np.arange(0, DC, 2, dtype=np.float32) / np.float32(DC))
                       .astype(np.float32))).astype(np.float32)
    freqs = np.arange(L, dtype=np.float32)[:, None] * inv_freq[None, :]
    sin = np.repeat(np.sin(freqs.astype(np.float64)), 2, axis=-1).astype(np.float32)
    cos = np.repeat(np.cos(freqs.astype(np.float64)), 2, axis=-1).astype(np.float32)
    sin[:, :DC // 2] = -sin[:, :DC // 2]
    return np.ascontiguousarray(np.stack([np.tile(cos.T, (2, 1)), np.tile(sin.T, (2, 1))], axis=1))


def layouts(v):
    x = v["x"]
    ctx = v["ctx_512"].reshape(BATCH * L, DC).T
    rot = np.concatenate([ctx[DC // 2:], ctx[:DC // 2]])

    def chunked(w):
        return w.reshape(-1, P, w.shape[1]).transpose(1, 0, 2)

    lat = v["L0_attn_latent_keys"]
    return {
        "x": x.reshape(TILES, P, D).transpose(1, 0, 2),
        "xT": x.reshape(BATCH, SEQ, KD, P).transpose(3, 0, 2, 1),
        "wqT1": chunked(v["L0_attn_Wq"].T), "wvT1": chunked(v["L0_attn_Wv"].T),
        "woT1": chunked(v["L0_attn_Wo"].T),
        "bqv": np.stack([v["L0_attn_bq"].reshape(KD, P).T, v["L0_attn_bv"].reshape(KD, P).T], 1),
        "bo": v["L0_attn_bo"].reshape(1, D),
        "latT": chunked(lat.T), "lat": lat.reshape(L, PAIRS, 2, HD),
        "ctxT": np.tile(np.stack([ctx, rot], 1), (2, 1, 1)),
        "wkrT": v["L0_xattn_W_kr"].transpose(2, 0, 1), "wqrT": v["L0_xattn_W_qr"].transpose(2, 0, 1),
        "wkcqT": v["L0_xattn_w_kc_q"].transpose(2, 0, 1),
        "wqx": v["L0_xattn_Wq"].reshape(H, HK, D).transpose(1, 0, 2),
        "wkckv": v["L0_xattn_w_kc_kv"].transpose(1, 0, 2),
        "woTx": v["L0_xattn_Wo"].T.reshape(H, HK, D).transpose(1, 0, 2),
        "w1T": chunked(v["L0_ffn_w1"].T), "w2T": chunked(v["L0_ffn_w2"].T),
        "w3T": chunked(v["L0_ffn_w3"].T),
        "g1": v["L0_ffn_g1"].reshape(1, D), "g2": v["L0_ffn_g2"].reshape(1, D),
        "g3": v["L0_ffn_g3"].reshape(1, FF),
        "rope": rope_tables(),
    }


def kernel(**inputs):
    import concourse.bacc as bacc
    from concourse.bass_utils import run_bass_kernel_spmd

    nc = bacc.Bacc("TRN2", target_bir_lowering=False, num_devices=1)
    arrays, args = {}, {}
    for name, value in layouts({k: np.asarray(v) for k, v in inputs.items()}).items():
        value = np.ascontiguousarray(value)
        arrays[f"in_{name}"] = value
        args[name] = nc.dram_tensor(f"in_{name}", value.shape, mybir.dt.from_np(value.dtype),
                                    kind="ExternalInput").ap()
    out = nc.dram_tensor("out_x", (TILES, P, D), F32, kind="ExternalOutput").ap()
    decoder_layer(nc, args, out)
    r = run_bass_kernel_spmd(nc, [arrays], core_ids=[0])
    return r.results[0]["out_x"].reshape(BATCH, SEQ, D)
```

```python
from contextlib import ExitStack

import numpy as np

import concourse.bass as bass
from concourse import mybir

ALU = mybir.AluOpType
ACT = mybir.ActivationFunctionType
AX = mybir.AxisListType.X
F32 = mybir.dt.float32
BF16 = mybir.dt.bfloat16

P = 128
D = 256
KD = D // P
BATCH, SEQ = 8, 256
TILES = BATCH * SEQ // P
H = 16
HD = D // H
L = 64
WIDE = H * L
PAIRS = H // 2
TOPK = 4
DC, RR, DCQ, HK = 64, 64, 192, 128
FF = 1024
FC = FF // P
LN_EPS, RMS_EPS, QUANT_MIN = 1e-5, 1e-8, 1e-4
ROUND = 12582912.0
QMAX = 127.0
HALF_ATANH = 0.5493061443340549
SLOTS = TILES + 5
LOOP_FROM, LOOP_TO = 3, 7


def decoder_layer(nc, a, out):
    with ExitStack() as ctx:
        def sb(name, shape, dt=F32):
            return ctx.enter_context(nc.sbuf_tensor(name, shape, dt))

        def sems(*names):
            return [ctx.enter_context(nc.semaphore(n)) for n in names]

        x_sb = sb("x_sb", [P, TILES, D])
        xT = sb("xT", [P, BATCH, KD, SEQ])
        wqT1 = sb("wqT1", [P, KD, D])
        wvT1 = sb("wvT1", [P, KD, D])
        woT1 = sb("woT1", [P, KD, D])
        bqv = sb("bqv", [P, 2, KD])
        bo_row = sb("bo_row", [P, D])
        lat_k = sb("lat_k", [P, KD, 4 * L])
        lat_v = sb("lat_v", [P, PAIRS, 2 * HD])
        ident = sb("ident", [P, P])
        ones = sb("ones", [P, P])
        minus_half = sb("minus_half", [P, 4])
        kv_bd = sb("kv_bd", [P, BATCH, P])
        ctx_raw = sb("ctx_raw", [P, 2, BATCH * L])
        rope_sb = sb("rope_sb", [P, 2, L])
        kv_cur = sb("kv_cur", [P, P])
        A_sb = sb("A_sb", [P, PAIRS, D])
        C_sb = sb("C_sb", [P, PAIRS, D])
        wkrT = sb("wkrT", [RR, H, DC])
        wkckv = sb("wkckv", [P, H, DC])
        T2 = sb("T2", [P, H * DC])
        tern12 = sb("tern12", [P, 2, KD, FF], BF16)
        tern3 = sb("tern3", [P, FC, D], BF16)
        g12 = sb("g12", [P, 2, D])
        g3 = sb("g3", [P, FF])
        region_q = sb("region_q", [P, H * D])
        wqx = region_q[:, :].rearrange("p (h d) -> p h d", h=H)
        woTx = region_q[:, :].rearrange("p (h d) -> p h d", h=H)
        region_c = sb("region_c", [P, 2 * H * HK])
        wkcqT_a = region_c[:, 0:H * HK].rearrange("p (h k) -> p h k", h=H)
        wkcqT_b = region_c[0:DCQ - P, H * HK:2 * H * HK].rearrange("p (h k) -> p h k", h=H)
        region_o = sb("region_o", [P, H * D])
        w12_raw = region_o[:, :].rearrange("p (w k f) -> p w k f", w=2, k=KD)
        th = region_o[:, 0:FF]
        hh = region_o[:, FF:2 * FF]
        hg = region_o[:, 2 * FF:3 * FF]
        junk_h = region_o[:, 3 * FF:4 * FF]
        region_r = sb("region_r", [P, H * DCQ])
        wqrT = region_r[0:RR, :].rearrange("p (h q) -> p h q", h=H)
        P2_even_odd = [region_r[:, 0:WIDE], region_r[:, 2 * WIDE:3 * WIDE]]
        PT2 = region_r[:, WIDE:2 * WIDE].rearrange("p (c t) -> p c t", c=PAIRS)
        region_t = sb("region_t", [P, 2 * WIDE])
        T1a, T1b = region_t[:, 0:WIDE], region_t[0:DCQ - P, WIDE:2 * WIDE]
        B_sb = region_t[:, :].rearrange("p (k n) -> p k n", k=KD)
        V_sb = sb("V_sb", [P, PAIRS, D])
        w3_raw = V_sb
        QT = sb("QT", [P, KD, SEQ])
        Ls = sb("Ls", [P, WIDE])
        mask = sb("mask", [P, WIDE])
        m8 = sb("m8", [P, H, 8])
        d4 = sb("d4", [P, H, TOPK])
        r1 = sb("r1", [P, 2, H])
        PT1 = sb("PT1", [P, PAIRS, P])
        AT = sb("AT", [P, KD, P])
        xb = sb("xb", [P, D])
        y = [sb(f"y{k}", [P, D]) for k in (1, 2, 3)]
        x1 = [sb(f"x1_{k}", [P, D]) for k in range(2)]
        x2 = [sb(f"x2_{k}", [P, D]) for k in range(2)]
        x3 = [sb(f"x3_{k}", [P, D]) for k in range(2)]
        x1T = sb("x1T", [P, KD, P])
        m2 = sb("m2", [P, H])
        r2 = sb("r2", [P, 2, H])
        stats = sb("stats", [P, 3, 6])
        moments = sb("moments", [P, 3, 2])
        spread = sb("spread", [P, 4])
        rstd = sb("rstd", [P, 4])
        xg = sb("xg", [P, 2, D])
        junk_x = sb("junk_x", [P, D])
        sqx = sb("sqx", [P, 4])
        amax = sb("amax", [P, 2])
        cq = sb("cq", [P, 2])
        icq = sb("icq", [P, 2])
        sq = sb("sq", [P, 2])
        dq = sb("dq", [P, 2])
        tq = sb("tq", [P, 2, 2])
        xqT = sb("xqT", [P, 2 * KD, P], BF16)
        sqh = sb("sqh", [P, 1])
        ch = sb("ch", [P, 4])
        dq3 = sb("dq3", [P, 2])
        hqT = sb("hqT", [P, FC, P], BF16)
        atanh_q = sb("atanh_q", [P, 3])
        prep = sb("prep", [P, 10, 3])

        wide = [ctx.enter_context(nc.psum_tensor(f"wide{k}", [P, WIDE], F32)) for k in range(3)]
        small = [ctx.enter_context(nc.psum_tensor(f"small{k}", [P, 512], F32)) for k in range(2)]

        ld_t, ld_s1, ld_back, ld_x, ld_ctx, ld_a, ld_c, ld_g, ld_raw, stored = sems(
            "ld_t", "ld_s1", "ld_back", "ld_x", "ld_ctx", "ld_a", "ld_c", "ld_g",
            "ld_raw", "stored")
        ld_xT = sems(*[f"ld_xT{b}" for b in range(BATCH)])
        c_zero, c_ident, c_const, c_kv, c_chain, c_tern, c_mean = sems(
            "c_zero", "c_ident", "c_const", "c_kv", "c_chain", "c_tern", "c_mean")
        pre_mm, pre_ev, pre_abs, pre_sum, pre_ln, pre_lnin = sems(
            "pre_mm", "pre_ev", "pre_abs", "pre_sum", "pre_ln", "pre_lnin")
        (p_QT, p_x1T, p_xqT, p_L1, p_L2, p_z1, p_z2, p_e0, p_e1, p_PT1, p_WT, p_hT, p_O1, p_PT2,
         p_O2, p_O3) = sems(*("p_QT p_x1T p_xqT p_L1 p_L2 p_z1 p_z2 p_e0 p_e1 p_PT1 p_WT p_hT p_O1 "
                              "p_PT2 p_O2 p_O3").split())
        (a_QT, a_x1T, a_xqT, a_L1, a_e4, a_tanh, a_exp1, a_exp2, a_sqh, a_e0, a_e1, a_sqx, a_PT1,
         a_AT, a_hT, a_PT2) = sems(*("a_QT a_x1T a_xqT a_L1 a_e4 a_tanh a_exp1 a_exp2 a_sqh a_e0 "
                                     "a_e1 a_sqx a_PT1 a_AT a_hT a_PT2").split())
        (v_y1, v_y2, v_y3, v_st1, v_st2, v_st3, v_mom, v_var, v_x1, v_x2, v_x3, v_max8, v_d4,
         v_mask, v_sum1, v_rec1, v_max2, v_sub2, v_sum2, v_rec2, v_u, v_h, v_amax, v_ms, v_cq,
         v_icq, v_sq, v_dq, v_tqh, v_tq, v_quant, v_amaxh, v_msh, v_cqh, v_icqh, v_sqh, v_dqh,
         v_quanth) = sems(*("v_y1 v_y2 v_y3 v_st1 v_st2 v_st3 v_mom v_var v_x1 v_x2 v_x3 v_max8 v_d4 "
                            "v_mask v_sum1 v_rec1 v_max2 v_sub2 v_sum2 v_rec2 v_u v_h v_amax v_ms "
                            "v_cq v_icq v_sq v_dq v_tqh v_tq v_quant v_amaxh v_msh v_cqh v_icqh "
                            "v_sqh v_dqh v_quanth").split())
        (g_rstd, g_xb, g_d1, g_mr, g_P1, g_kv, g_xg, g_rx, g_hg, g_P2) = sems(
            *"g_rstd g_xb g_d1 g_mr g_P1 g_kv g_xg g_rx g_hg g_P2".split())

        def since(eng, sem, count):
            if not isinstance(count, int) or count > 0:
                eng.wait_ge(sem, count)

        def on(n, total=TILES):
            return not isinstance(n, int) or 0 <= n < total

        def upto(n, total=TILES):
            return min(n, total) if isinstance(n, int) else n

        def bank_free(eng, steady, *idle):
            for sem, count in (steady, *idle) if isinstance(steady[1], int) else (steady,):
                since(eng, sem, upto(count))

        def run(eng, slot, after={}):
            for t in range(2 * LOOP_FROM):
                slot(t // 2, t % 2)
                if t in after:
                    after[t]()
            with eng.Fori(LOOP_FROM, LOOP_TO) as i:
                slot(i, 0), slot(i, 1)
            for t in range(2 * LOOP_TO, SLOTS):
                slot(t // 2, t % 2)

        def heads(ap):
            return ap.rearrange("p (h l) -> p h l", h=H)

        def over_heads(column):
            return column.to_broadcast([P, H, L])

        block = ctx.enter_context(nc.Block())

        @block.sync
        def _(sp):
            sp.dma_start(wkrT[:], a["wkrT"]).then_inc(ld_t, 16)
            sp.dma_start(wqrT, a["wqrT"]).then_inc(ld_t, 16)
            sp.dma_start(wkcqT_a, a["wkcqT"][0:P]).then_inc(ld_t, 16)
            sp.dma_start(wkcqT_b, a["wkcqT"][P:DCQ]).then_inc(ld_t, 16)
            sp.dma_start(w12_raw[:, 0], a["w1T"]).then_inc(ld_raw, 16)
            sp.dma_start(w12_raw[:, 1], a["w2T"]).then_inc(ld_raw, 16)
            sp.dma_start(w3_raw[:], a["w3T"]).then_inc(ld_raw, 16)
            sp.dma_start(wqT1[:], a["wqT1"]).then_inc(ld_s1, 16)
            sp.dma_start(xT[:, 0], a["xT"][:, 0]).then_inc(ld_xT[0], 16)
            sp.dma_start(bqv[:], a["bqv"]).then_inc(ld_s1, 16)
            sp.wait_ge(c_zero, 2)
            for q in range(P // HD):
                sp.dma_start(lat_k[HD * q:HD * (q + 1), :, L * (q % 4):L * (q % 4 + 1)],
                             a["latT"][HD * q:HD * (q + 1)]).then_inc(ld_s1, 16)
            for e in range(2):
                sp.dma_start(lat_v[L * e:L * (e + 1), :, HD * e:HD * (e + 1)],
                             a["lat"][:, :, e]).then_inc(ld_s1, 16)
            sp.dma_start(wqx, a["wqx"]).then_inc(ld_a, 16)
            sp.dma_start(ctx_raw[:], a["ctxT"]).then_inc(ld_ctx, 16)
            sp.dma_start(rope_sb[:], a["rope"]).then_inc(ld_ctx, 16)
            sp.dma_start(wvT1[:], a["wvT1"]).then_inc(ld_back, 16)
            sp.dma_start(woT1[:], a["woT1"]).then_inc(ld_back, 16)
            sp.dma_start(bo_row[:], a["bo"].to_broadcast([P, D])).then_inc(ld_back, 16)
            sp.dma_start(xT[:, 1], a["xT"][:, 1]).then_inc(ld_xT[1], 16)
            sp.dma_start(x_sb[:, 0:2], a["x"][:, 0:2]).then_inc(ld_x, 16)
            sp.dma_start(x_sb[:, 2:TILES], a["x"][:, 2:TILES]).then_inc(ld_x, 16)
            sp.dma_start(wkckv[:], a["wkckv"]).then_inc(ld_c, 16)
            sp.wait_ge(pre_mm, 4)
            sp.dma_start(woTx, a["woTx"]).then_inc(ld_c, 16)
            for b in range(2, 4):
                sp.dma_start(xT[:, b], a["xT"][:, b]).then_inc(ld_xT[b], 16)
            for k, name in enumerate(("g1", "g2")):
                sp.dma_start(g12[:, k, :], a[name].to_broadcast([P, D])).then_inc(ld_g, 16)
            sp.dma_start(g3[:], a["g3"].to_broadcast([P, FF])).then_inc(ld_g, 16)
            for b in range(4, BATCH):
                sp.dma_start(xT[:, b], a["xT"][:, b]).then_inc(ld_xT[b], 16)

            def slot(i, p):
                b3 = 2 * i + p - 5
                if on(b3):
                    sp.wait_ge(v_x3, b3 + 1)
                    sp.dma_start(out[b3], x3[1 - p][:]).then_inc(stored, 16)

            run(sp, slot)
            sp.wait_ge(stored, 16 * TILES)

        @block.tensor
        def _(pe):
            def project_q(b):
                for g in range(KD):
                    for k in range(KD):
                        mm = pe.matmul(small[1][:, g * SEQ:(g + 1) * SEQ],
                                       wqT1[:, k, g * P:(g + 1) * P], xT[:, b, k, :],
                                       start=(k == 0), stop=(k == KD - 1))
                mm.then_inc(p_QT, 1)

            def slot(i, p):
                t = 2 * i + p
                n1, n2, n3, b1, b2, b3, q = t, t - 2, t - 4, t - 1, t - 3, t - 5, 1 - p
                if isinstance(i, int) and p == 0 and i < BATCH:
                    pe.wait_ge(ld_xT[i], 16)
                if on(b1):
                    bank_free(pe, (v_y2, b2), (v_y3, b3), (a_AT, b1))
                    for g in range(KD):
                        for k in range(KD):
                            pe.matmul(small[0][:, g * P:(g + 1) * P], wvT1[:, k, g * P:(g + 1) * P],
                                      xT[:, i - q, k, q * P:(q + 1) * P],
                                      start=(g == 0 and k == 0), stop=False, skip_group_check=True)
                    pe.wait_ge(g_P1, b1 + 1)
                    bank_free(pe, (v_h, b3 + 1), (v_sub2, n2), (a_PT1, b1))
                    for c in range(PAIRS):
                        mm = pe.transpose(wide[0][:, c * P:(c + 1) * P], Ls[:, c * P:(c + 1) * P],
                                          ident[:])
                    mm.then_inc(p_PT1, 1)
                if on(n1):
                    pe.wait_ge(a_QT, i + 1)
                    bank_free(pe, (a_e0, upto(t - 1, 2 * BATCH)), (a_PT2, b2), (a_L1, n1))
                    for g in range(KD):
                        for j in range(2):
                            mm = pe.matmul(wide[1][:, j * 512 + g * SEQ:j * 512 + (g + 1) * SEQ],
                                           QT[j * L:(j + 1) * L, g, p * P:(p + 1) * P],
                                           lat_k[j * L:(j + 1) * L, g, :], start=True, stop=True)
                    mm.then_inc(p_L1, 1)
                if on(n2):
                    pe.wait_ge(v_x1, n2 + 1)
                    if p == 0:
                        bank_free(pe, (a_QT, upto(i + 1, BATCH)), (a_xqT, n3), (v_y1, b1))
                    else:
                        bank_free(pe, (a_xqT, n3), (v_y1, b1), (a_QT, upto(i + 1, BATCH)))
                    for k in range(KD):
                        mm = pe.transpose(small[1][:, k * P:(k + 1) * P],
                                          x1[p][:, k * P:(k + 1) * P], ident[:])
                    mm.then_inc(p_x1T, 1)
                if on(b1):
                    pe.wait_ge(a_PT1, b1 + 1)
                    for c in range(PAIRS):
                        g, r = divmod(c, PAIRS // KD)
                        mm = pe.matmul(small[0][32 * r:32 * (r + 1), g * P:(g + 1) * P],
                                       lat_v[:, c, :], PT1[:, c, :],
                                       start=False, stop=(c == PAIRS - 1), skip_group_check=True)
                    mm.then_inc(p_WT, 1)
                if on(b3):
                    pe.wait_ge(v_quanth, b3 + 1)
                    bank_free(pe, (a_e1, upto(t - 1, 2 * BATCH)), (v_u, n3), (a_hT, b3))
                    for c in range(FC):
                        mm = pe.transpose(wide[2][:, c * P:(c + 1) * P], hg[:, c * P:(c + 1) * P],
                                          ident[:])
                    mm.then_inc(p_hT, 1)
                if on(n2):
                    pe.wait_ge(a_x1T, n2 + 1)
                    pe.wait_ge(a_e1, 2 * i - 1)
                    bank_free(pe, (a_PT1, b1 + 1), (v_h, n3), (v_sub2, n2))
                    for r in range(2):
                        for k in range(KD):
                            mm = pe.matmul(wide[0][:, r * 512:(r + 1) * 512], x1T[:, k, :],
                                           B_sb[:, k, r * 512:(r + 1) * 512],
                                           start=(k == 0), stop=(k == KD - 1))
                    mm.then_inc(p_L2, 1)
                if on(b1):
                    pe.wait_ge(a_AT, b1 + 1)
                    bank_free(pe, (a_x1T, n2 + 1), (a_xqT, n3), (v_y1, b1),
                              (a_QT, upto(i + 1, BATCH)))
                    for g in range(KD):
                        mm = pe.matmul(small[1][:, 0:D], AT[:, g, :], woT1[:, g, :],
                                       start=(g == 0), stop=(g == KD - 1))
                    mm.then_inc(p_O1, 1)
                if on(b3):
                    pe.wait_ge(a_hT, b3 + 1)
                    bank_free(pe, (a_AT, b1 + 1), (v_y2, b2), (v_y3, b3))
                    for c in range(FC):
                        mm = pe.matmul(small[0][:, 0:D], hqT[:, c, :], tern3[:, c, :],
                                       start=(c == 0), stop=(c == FC - 1))
                    mm.then_inc(p_O3, 1)
                if on(n3):
                    pe.wait_ge(v_quant, n3 + 1)
                    bank_free(pe, (v_y1, b1 + 1), (a_x1T, n2 + 1), (a_xqT, n3),
                              (a_QT, upto(i + 1, BATCH)))
                    for k in range(2 * KD):
                        mm = pe.transpose(small[1][:, k * P:(k + 1) * P],
                                          xg[:, k // KD, (k % KD) * P:(k % KD + 1) * P], ident[:])
                    mm.then_inc(p_xqT, 1)
                if on(b2):
                    pe.wait_ge(g_P2, b2 + 1)
                    bank_free(pe, (a_L1, n1 + 1), (a_e0, upto(t - 1, 2 * BATCH)), (a_PT2, b2))
                    for c in range(PAIRS):
                        mm = pe.transpose(wide[1][:, c * P:(c + 1) * P],
                                          P2_even_odd[q][:, c * P:(c + 1) * P],
                                          ident[:])
                    mm.then_inc(p_PT2, 1)
                if on(n3):
                    pe.wait_ge(a_xqT, n3 + 1)
                    bank_free(pe, (a_hT, b3 + 1), (a_e1, upto(t - 1, 2 * BATCH)), (v_u, n3))
                    for w, sem in enumerate((p_z1, p_z2)):
                        if w == 1:
                            bank_free(pe, (v_sub2, n2 + 1), (a_PT1, b1 + 1), (v_h, n3))
                        for r in range(2):
                            for k in range(KD):
                                mm = pe.matmul(wide[2 - 2 * w][:, r * 512:(r + 1) * 512],
                                               xqT[:, w * KD + k, :],
                                               tern12[:, w, k, r * 512:(r + 1) * 512],
                                               start=(k == 0), stop=(k == KD - 1))
                        mm.then_inc(sem, 1)
                if on(b2):
                    pe.wait_ge(a_PT2, b2 + 1)
                    pe.wait_ge(a_e1, 2 * (i - q))
                    bank_free(pe, (v_y3, b3 + 1), (a_AT, b1 + 1), (v_y2, b2))
                    for c in range(PAIRS):
                        mm = pe.matmul(small[0][:, 0:D], PT2[:, c, :], V_sb[:, c, :],
                                       start=(c == 0), stop=(c == PAIRS - 1))
                    mm.then_inc(p_O2, 1)
                if p == 0 and on(i - 1, BATCH):
                    pe.wait_ge(g_kv, i)
                    bank_free(pe, (a_PT2, b2 + 1), (a_L1, n1 + 1), (a_e0, t - 1))
                    bank_free(pe, (v_u, n3 + 1), (a_hT, b3 + 1), (a_e1, t - 1))
                    for half, sem in enumerate((p_e0, p_e1)):
                        for c in range(PAIRS // 2):
                            mm = pe.matmul(wide[1 + half][:, c * D:(c + 1) * D], kv_cur[:],
                                           C_sb[:, half * PAIRS // 2 + c, :], start=True, stop=True)
                        mm.then_inc(sem, 1)
                if p == 1 and on(i, BATCH):
                    bank_free(pe, (a_PT2, b2 + 1), (a_L1, n1 + 1), (a_e0, t - 1))
                    bank_free(pe, (v_u, n3 + 1), (a_hT, b3 + 1), (a_e1, t - 1))
                    for k, sem in enumerate((p_e0, p_e1)):
                        for c in range(PAIRS):
                            mm = pe.matmul(wide[1 + k][:, c * P:(c + 1) * P],
                                           A_sb[:, c, k * P:(k + 1) * P], kv_bd[:, i, :],
                                           start=True, stop=True)
                        mm.then_inc(sem, 1)
                if p == 1 and on(i + 1, BATCH):
                    if isinstance(i, int):
                        pe.wait_ge(ld_xT[i + 1], 16)
                    bank_free(pe, (a_xqT, n3 + 1), (v_y1, b1 + 1), (a_x1T, n2 + 1), (a_QT, i + 1))
                    project_q(i + 1)

            def side_weights():
                pe.wait_ge(ld_t, 16 * 4)
                for half, (lo, hi) in enumerate(((0, P), (P, DCQ))):
                    for h in range(H):
                        mm = pe.matmul(wide[1 + half][0:hi - lo, h * DC:(h + 1) * DC],
                                       wqrT[:, h, lo:hi], wkrT[:, h, :], start=True, stop=True)
                    mm.then_inc(pre_mm, 1)
                pe.wait_ge(pre_ev, 2)
                for h in range(H):
                    if h == H // 2:
                        ffn_sums()
                    pe.matmul(wide[0][:, h * DC:(h + 1) * DC], wkcqT_a[:, h, :],
                              T1a[:, h * DC:(h + 1) * DC], start=True, stop=False)
                    mm = pe.matmul(wide[0][:, h * DC:(h + 1) * DC], wkcqT_b[:, h, :],
                                   T1b[:, h * DC:(h + 1) * DC], start=False, stop=True)
                mm.then_inc(pre_mm, 1)
            def score_weights():
                pe.wait_ge(ld_a, 16)
                pe.wait_ge(a_L1, 1)
                pe.wait_ge(pre_ev, 3)
                for h in range(H):
                    c, e = divmod(h, 2)
                    mm = pe.matmul(wide[1 + c // 4][DC * e:DC * (e + 1), (c % 4) * D:(c % 4 + 1) * D],
                                   T2[:, h * DC:(h + 1) * DC], wqx[:, h, :], start=True, stop=True)
                mm.then_inc(pre_mm, 1)
                pe.wait_ge(pre_ev, 5)
                pe.wait_ge(c_mean, 1)
                pe.wait_ge(c_kv, 1)

            def output_weights():
                pe.wait_ge(ld_c, 16 * 2)
                for half in range(2):
                    pe.wait_ge((a_PT1, a_e0)[half], 1)
                    for h in range(half * H // 2, (half + 1) * H // 2):
                        c, e = divmod(h, 2)
                        mm = pe.matmul(wide[half][DC * e:DC * (e + 1), (c % 4) * D:(c % 4 + 1) * D],
                                       wkckv[:, h, :], woTx[:, h, :], start=True, stop=True)
                    mm.then_inc(pre_mm, 1)
                pe.wait_ge(pre_ev, 7)

            def ffn_sums():
                pe.wait_ge(c_const, 3)
                pe.wait_ge(pre_abs, 3)
                pe.matmul(small[0][:, 0:3], ones[:], prep[:, 0, :], start=True, stop=True
                          ).then_inc(pre_sum, 1)

            def first_weights():
                score_weights()
                pe.wait_ge(ld_back, 16 * 3)
                pe.wait_ge(c_ident, 1)

            side_weights()
            pe.wait_ge(ld_s1, 16 * 12)
            pe.wait_ge(ld_xT[0], 16)
            project_q(0)
            def loop_loads():
                pe.wait_ge(c_tern, 3)
                for b in range(LOOP_FROM, LOOP_TO + 1):
                    pe.wait_ge(ld_xT[b], 16)

            run(pe, slot, {0: first_weights, 1: output_weights, 3: loop_loads})

        @block.scalar
        def _(act):
            def copy_q(b):
                act.wait_ge(p_QT, b + 1)
                for g in range(KD):
                    ins = act.activation(QT[:, g, :], small[1][:, g * SEQ:(g + 1) * SEQ],
                                         ACT.Identity, bias=bqv[:, 0, g:g + 1])
                ins.then_inc(a_QT, 1)

            def slot(i, p):
                t = 2 * i + p
                n1, n2, n3, b1, b2, b3, q = t, t - 2, t - 4, t - 1, t - 3, t - 5, 1 - p
                if on(b1):
                    act.wait_ge(p_PT1, b1 + 1)
                    since(act, p_WT, b1)
                    act.activation(PT1[:], wide[0][:].rearrange("p (c t) -> p c t", c=PAIRS),
                                   ACT.Copy).then_inc(a_PT1, 1)
                if on(n1):
                    act.wait_ge(p_L1, n1 + 1)
                    since(act, p_PT1, n1)
                    for j in range(2):
                        ins = act.activation(
                            Ls[:].rearrange("p (g j n) -> p j g n", g=KD, j=2)[:, j],
                            wide[1][:, j * 512:(j + 1) * 512].rearrange("p (g n) -> p g n", g=KD),
                            ACT.Copy)
                    ins.then_inc(a_L1, 1)
                if on(n2):
                    act.wait_ge(p_x1T, n2 + 1)
                    since(act, p_L2, n2)
                    act.activation(x1T[:], small[1][:, 0:D].rearrange("p (k t) -> p k t", k=KD),
                                   ACT.Copy).then_inc(a_x1T, 1)
                if on(b1):
                    act.wait_ge(p_WT, b1 + 1)
                    since(act, p_O1, b1)
                    for g in range(KD):
                        ins = act.activation(AT[:, g, :], small[0][:, g * P:(g + 1) * P],
                                             ACT.Identity, bias=bqv[:, 1, g:g + 1])
                    ins.then_inc(a_AT, 1)
                if on(b3):
                    act.wait_ge(p_hT, b3 + 1)
                    since(act, p_O3, b3)
                    act.activation(hqT[:], wide[2][:].rearrange("p (c t) -> p c t", c=FC),
                                   ACT.Copy, bias=-ROUND).then_inc(a_hT, 1)
                if on(n1):
                    act.wait_ge(v_d4, n1 + 1)
                    act.activation(d4[:], d4[:], ACT.Exp, scale=HD ** -0.5).then_inc(a_e4, 1)
                    act.wait_ge(g_d1, n1 + 1)
                    act.activation(Ls[:], Ls[:], ACT.Exp, scale=HD ** -0.5).then_inc(a_exp1, 1)
                if on(n3):
                    act.wait_ge(p_xqT, n3 + 1)
                    since(act, p_z2, n3)
                    act.activation(xqT[:], small[1][:].rearrange("p (k t) -> p k t", k=2 * KD),
                                   ACT.Copy, bias=-ROUND).then_inc(a_xqT, 1)
                if on(n2):
                    act.wait_ge(v_sub2, n2 + 1)
                    act.activation(P2_even_odd[p], P2_even_odd[p], ACT.Exp).then_inc(a_exp2, 1)
                if on(b2):
                    act.wait_ge(p_PT2, b2 + 1)
                    since(act, p_O2, b2)
                    act.activation(PT2, wide[1][:].rearrange("p (c t) -> p c t", c=PAIRS),
                                   ACT.Copy).then_inc(a_PT2, 1)
                if on(n3):
                    act.wait_ge(p_z1, n3 + 1)
                    act.wait_ge(v_tq, n3 + 1)
                    since(act, v_h, n3)
                    act.activation(th, wide[2][:], ACT.Tanh, scale=tq[:, p, 0:1]).then_inc(a_tanh, 1)
                    act.wait_ge(v_h, n3 + 1)
                    since(act, a_sqh, n3)
                    act.activation(junk_h, hh, ACT.Square, accum_out=sqh[:]).then_inc(a_sqh, 1)
                copy_spare(i, p, 0)
                if on(b2):
                    act.wait_ge(v_x2, b2 + 1)
                    since(act, a_sqx, b2)
                    act.activation(junk_x[:], x2[q][:], ACT.Square,
                                   accum_out=sqx[:, 0:1]).then_inc(a_sqx, 1)
                copy_spare(i, p, 1)
                if p == 1 and on(i + 1, BATCH):
                    copy_q(i + 1)

            def copy_spare(i, p, half):
                ready, copied = ((p_e0, a_e0), (p_e1, a_e1))[half]
                if p == 0 and on(i - 1, BATCH):
                    act.wait_ge(ready, 2 * i)
                    since(act, p_O2, 2 * i - 3)
                    act.activation(V_sb[:, half * 4:(half + 1) * 4, :],
                                   wide[1 + half][:].rearrange("p (c n) -> p c n", c=4),
                                   ACT.Copy).then_inc(copied, 1)
                if p == 1 and on(i, BATCH):
                    act.wait_ge(ready, 2 * i + 1)
                    act.activation(B_sb[:, half, :], wide[1 + half][:], ACT.Copy
                                   ).then_inc(copied, 1)

            def side_weights():
                act.wait_ge(pre_mm, 1)
                act.activation(T1a, wide[1][:], ACT.Copy).then_inc(pre_ev, 1)
                act.wait_ge(pre_mm, 2)
                act.activation(T1b, wide[2][0:DCQ - P, :], ACT.Copy).then_inc(pre_ev, 1)
                ffn_sums()
                act.wait_ge(pre_mm, 3)
                act.activation(T2[:], wide[0][:], ACT.Copy).then_inc(pre_ev, 1)

            def score_weights():
                act.wait_ge(pre_mm, 4)
                for half in range(2):
                    act.activation(A_sb[:, 4 * half:4 * half + 4, :],
                                   wide[1 + half][:].rearrange("p (c n) -> p c n", c=4),
                                   ACT.Copy).then_inc(pre_ev, 1)

            def output_weights():
                for half in range(2):
                    act.wait_ge(pre_mm, 5 + half)
                    act.activation(C_sb[:, 4 * half:4 * half + 4, :],
                                   wide[half][:].rearrange("p (c n) -> p c n", c=4),
                                   ACT.Copy).then_inc(pre_ev, 1)

                act.wait_ge(c_tern, 3)

            def ffn_sums():
                act.wait_ge(ld_raw, 16 * 3)
                for w in range(2):
                    act.activation(tern12[:, w].rearrange("p k f -> p (k f)"),
                                   w12_raw[:, w].rearrange("p k f -> p (k f)"), ACT.Abs,
                                   accum_out=prep[:, 0, w:w + 1]).then_inc(pre_abs, 1)
                act.activation(tern3[:].rearrange("p c d -> p (c d)"),
                               w3_raw[:].rearrange("p c d -> p (c d)"), ACT.Abs,
                               accum_out=prep[:, 0, 2:3]).then_inc(pre_abs, 1)
                act.wait_ge(pre_lnin, 1)
                act.activation(prep[:, 5, :], prep[:, 4, :], ACT.Ln).then_inc(pre_ln, 1)

            side_weights()
            act.wait_ge(ld_s1, 16 * 12)
            copy_q(0)
            run(act, slot, {0: score_weights, 1: output_weights})

        @block.vector
        def _(dve):
            def moments_of(k, n, sem_y, sem_st):
                dve.wait_ge(sem_y, n + 1)
                dve.bn_stats(stats[:, k, :], y[k][:]).then_inc(sem_st, 1)
                dve.wait_ge(c_zero, 3)
                dve.wait_ge(sem_st, n + 1)
                dve.bn_aggr(moments[:, k, :], stats[:, k, :]).then_inc(v_mom, 1)

            def slot(i, p):
                t = 2 * i + p
                n1, n2, n3, b1, b2, b3, q = t, t - 2, t - 4, t - 1, t - 3, t - 5, 1 - p
                if on(n1):
                    dve.wait_ge(a_L1, n1 + 1)
                    since(dve, g_d1, n1)
                if on(n3):
                    dve.wait_ge(v_sq, n3 + 1)
                    for k in range(2):
                        ins = dve.tensor_scalar(xg[:, k, :], xg[:, k, :], sq[:, k:k + 1], ROUND,
                                                ALU.mult, ALU.add)
                    ins.then_inc(v_quant, 1)
                if on(n1):
                    for h in range(H):
                        ins = dve.max(m8[:, h, :], Ls[:, h * L:(h + 1) * L])
                    ins.then_inc(v_max8, 1)
                    dve.wait_ge(v_max8, n1 + 1)
                    dve.tensor_tensor(d4[:], m8[:, :, 0:TOPK],
                                      m8[:, :, 0:1].to_broadcast([P, H, TOPK]), ALU.subtract
                                      ).then_inc(v_d4, 1)
                    since(dve, g_P1, n1)
                    dve.tensor_tensor(heads(mask[:]), heads(Ls[:]),
                                      over_heads(m8[:, :, TOPK - 1:TOPK]), ALU.is_ge
                                      ).then_inc(v_mask, 1)
                    dve.wait_ge(a_e4, n1 + 1)
                    dve.tensor_reduce(r1[:, 0, :], d4[:], AX, ALU.add).then_inc(v_sum1, 1)
                    dve.wait_ge(v_sum1, n1 + 1)
                    since(dve, g_mr, n1)
                    dve.reciprocal(r1[:, 1, :], r1[:, 0, :]).then_inc(v_rec1, 1)
                if on(n2):
                    dve.wait_ge(p_L2, n2 + 1)
                    dve.tensor_reduce(m2[:], heads(wide[0][:]), AX, ALU.max).then_inc(v_max2, 1)
                if on(b1):
                    dve.wait_ge(p_O1, b1 + 1)
                    dve.wait_ge(g_xb, b1 + 1)
                    since(dve, v_x1, b1)
                    dve.tensor_tensor(y[0][:], small[1][:, 0:D], xb[:], ALU.add).then_inc(v_y1, 1)
                if on(n2):
                    dve.wait_ge(v_max2, n2 + 1)
                    since(dve, p_PT2, n2 - 1)
                    dve.tensor_tensor(heads(P2_even_odd[p]), heads(wide[0][:]),
                                      over_heads(m2[:].rearrange("p (h o) -> p h o", o=1)),
                                      ALU.subtract).then_inc(v_sub2, 1)
                if on(b3):
                    dve.wait_ge(p_O3, b3 + 1)
                    dve.wait_ge(v_dqh, b3 + 1)
                    since(dve, v_x3, b3)
                    dve.scalar_tensor_tensor(y[2][:], small[0][:, 0:D], dq3[:, q:q + 1], x2[q][:],
                                             ALU.mult, ALU.add).then_inc(v_y3, 1)
                if on(b1):
                    moments_of(0, b1, v_y1, v_st1)
                if on(b3):
                    moments_of(2, b3, v_y3, v_st3)
                if on(n3):
                    dve.wait_ge(a_tanh, n3 + 1)
                    dve.scalar_tensor_tensor(th, th, 1.0, wide[2][:], ALU.add, ALU.mult
                                             ).then_inc(v_u, 1)
                    dve.wait_ge(v_u, n3 + 1)
                    dve.wait_ge(p_z2, n3 + 1)
                    since(dve, a_sqh, n3)
                    since(dve, g_hg, n3)
                    dve.scalar_tensor_tensor(hh, wide[0][:], tq[:, p, 1:2], th, ALU.mult, ALU.mult
                                             ).then_inc(v_h, 1)
                if on(n2):
                    dve.wait_ge(a_exp2, n2 + 1)
                    dve.tensor_reduce(r2[:, 0, :], heads(P2_even_odd[p]), AX, ALU.add).then_inc(v_sum2, 1)
                    dve.wait_ge(v_sum2, n2 + 1)
                    dve.reciprocal(r2[:, 1, :], r2[:, 0, :]).then_inc(v_rec2, 1)
                if on(n3):
                    dve.wait_ge(a_sqh, n3 + 1)
                    dve.tensor_scalar(spread[:, 3:4], sqh[:], 1.0 / FF, RMS_EPS, ALU.mult, ALU.add
                                      ).then_inc(v_msh, 1)
                if on(b2):
                    dve.wait_ge(p_O2, b2 + 1)
                    since(dve, v_x2, b2)
                    dve.tensor_tensor(y[1][:], small[0][:, 0:D], x1[q][:], ALU.add).then_inc(v_y2, 1)
                    moments_of(1, b2, v_y2, v_st2)
                if on(b1) or on(b2) or on(b3):
                    made = sum(max(0, upto(n + 1)) for n in (b1, b2, b3)) \
                        if isinstance(t, int) else 3 * t - 6
                    dve.wait_ge(v_mom, made)
                    dve.tensor_scalar(spread[:, 0:3], moments[:, :, 1], LN_EPS, None, ALU.add
                                      ).then_inc(v_var, 1)
                if on(n3):
                    dve.wait_ge(g_hg, n3 + 1)
                    dve.tensor_reduce(ch[:, 0:1], hg, AX, ALU.max, apply_absolute_value=True
                                      ).then_inc(v_amaxh, 1)
                if on(b1) or on(b2) or on(b3):
                    dve.wait_ge(g_rstd, t)
                for k, (n, dst, sem) in enumerate(((b1, x1, v_x1), (b2, x2, v_x2), (b3, x3, v_x3))):
                    if on(n):
                        if k == 0:
                            since(dve, p_x1T, n - 1)
                        if k == 2:
                            since(dve, stored, 16 * n)
                        dve.tensor_scalar(dst[q][:], y[k][:], moments[:, k, 0:1], rstd[:, k:k + 1],
                                          ALU.subtract, ALU.mult).then_inc(sem, 1)
                if on(n3):
                    dve.wait_ge(v_amaxh, n3 + 1)
                    dve.tensor_scalar(ch[:, 1:2], ch[:, 0:1], rstd[:, 3:4], QUANT_MIN, ALU.mult,
                                      ALU.max).then_inc(v_cqh, 1)
                    dve.wait_ge(v_cqh, n3 + 1)
                    dve.reciprocal(ch[:, 2:3], ch[:, 1:2]).then_inc(v_icqh, 1)
                    dve.tensor_tensor(dq3[:, p:p + 1], ch[:, 1:2], atanh_q[:, 2:3], ALU.mult
                                      ).then_inc(v_dqh, 1)
                    dve.wait_ge(v_icqh, n3 + 1)
                    dve.tensor_scalar(ch[:, 3:4], ch[:, 2:3], rstd[:, 3:4], QMAX, ALU.mult, ALU.mult
                                      ).then_inc(v_sqh, 1)
                    dve.wait_ge(v_sqh, n3 + 1)
                    dve.tensor_scalar(hg, hg, ch[:, 3:4], ROUND, ALU.mult, ALU.add
                                      ).then_inc(v_quanth, 1)
                if on(b2):
                    dve.wait_ge(a_sqx, b2 + 1)
                    dve.tensor_scalar(sqx[:, 1:2], sqx[:, 0:1], 1.0 / D, RMS_EPS, ALU.mult, ALU.add
                                      ).then_inc(v_ms, 1)
                    dve.wait_ge(g_xg, b2 + 1)
                    dve.tensor_reduce(amax[:], xg[:], AX, ALU.max, apply_absolute_value=True
                                      ).then_inc(v_amax, 1)
                    dve.wait_ge(v_amax, b2 + 1)
                    dve.wait_ge(g_rx, b2 + 1)
                    dve.tensor_scalar(cq[:], amax[:], sqx[:, 2:3], QUANT_MIN, ALU.mult, ALU.max
                                      ).then_inc(v_cq, 1)
                    dve.wait_ge(v_cq, b2 + 1)
                    dve.reciprocal(icq[:], cq[:]).then_inc(v_icq, 1)
                    dve.tensor_tensor(dq[:], cq[:], atanh_q[:, 0:2], ALU.mult).then_inc(v_dq, 1)
                    dve.wait_ge(v_icq, b2 + 1)
                    dve.tensor_scalar(sq[:], icq[:], sqx[:, 2:3], QMAX, ALU.mult, ALU.mult
                                      ).then_inc(v_sq, 1)
                    dve.wait_ge(v_dq, b2 + 1)
                    dve.tensor_scalar(tq[:, q, 0:1], dq[:, 0:1], 0.5, None, ALU.mult
                                      ).then_inc(v_tqh, 1)
                    dve.wait_ge(v_tqh, b2 + 1)
                    dve.tensor_tensor(tq[:, q, 1:2], tq[:, q, 0:1], dq[:, 1:2], ALU.mult
                                      ).then_inc(v_tq, 1)

            chain = [0]

            def link(ins):
                chain[0] += 1
                ins.then_inc(c_chain, 1)
                dve.wait_ge(c_chain, chain[0])

            def atanh_weights():
                dve.wait_ge(pre_sum, 1)
                mean, one_m, ratio, ln_in, ln_out = (prep[:, k, :] for k in (1, 2, 3, 4, 5))
                sq_, acc, small_s, low = (prep[:, k, :] for k in (6, 7, 8, 9))
                dve.tensor_scalar(mean, small[0][:, 0:3], 1.0 / (D * FF), None, ALU.mult
                                  ).then_inc(c_mean, 1)
                dve.wait_ge(c_mean, 1)
                link(dve.tensor_scalar(one_m, mean, -1.0, 1.0, ALU.mult, ALU.add))
                link(dve.reciprocal(ratio, one_m))
                link(dve.scalar_tensor_tensor(ln_in, mean, 1.0, ratio, ALU.add, ALU.mult))
                dve.tensor_tensor(sq_, mean, mean, ALU.mult).then_inc(pre_lnin, 1)
                dve.wait_ge(pre_lnin, 1)
                link(dve.tensor_scalar(acc, sq_, 1.0 / 17.0, None, ALU.mult))
                for k in (15, 13, 11, 9, 7, 5, 3):
                    link(dve.scalar_tensor_tensor(acc, acc, 1.0 / k, sq_, ALU.add, ALU.mult))
                link(dve.scalar_tensor_tensor(acc, acc, 1.0, mean, ALU.add, ALU.mult))
                link(dve.tensor_scalar(low, mean, 0.25, None, ALU.is_lt))
                dve.wait_ge(pre_ln, 1)
                link(dve.tensor_scalar(small_s, ln_out, 0.5, None, ALU.mult))
                link(dve.tensor_tensor(acc, acc, small_s, ALU.subtract))
                link(dve.tensor_tensor(acc, acc, low, ALU.mult))
                link(dve.tensor_tensor(acc, acc, small_s, ALU.add))
                link(dve.tensor_scalar(atanh_q[:], acc, 1.0 / QMAX, None, ALU.mult))
                link(dve.tensor_scalar(small_s, mean, RMS_EPS, HALF_ATANH, ALU.add, ALU.mult))
                link(dve.tensor_scalar(low, small_s, -1.0, None, ALU.mult))

            def ternary_weights():
                for w, (raw, dst) in enumerate(((w12_raw[:, 0], tern12[:, 0]),
                                                (w12_raw[:, 1], tern12[:, 1]), (w3_raw[:], tern3[:]))):
                    raw, dst = (v.rearrange("p a b -> p (a b)") for v in (raw, dst))
                    link(dve.tensor_scalar(dst, raw, prep[:, 9, w:w + 1], None, ALU.is_lt))
                    dve.scalar_tensor_tensor(dst, raw, prep[:, 8, w:w + 1], dst, ALU.is_gt,
                                             ALU.subtract).then_inc(c_tern, 1)

            def rope():
                dve.wait_ge(ld_ctx, 16 * 2)
                ctx3 = [ctx_raw[:, r, :].rearrange("p (b l) -> p b l", b=BATCH) for r in range(2)]
                for r in range(2):
                    table = rope_sb[:, r:r + 1, :].to_broadcast([P, BATCH, L])
                    link(dve.tensor_tensor(ctx3[r], ctx3[r], table, ALU.mult))
                dve.wait_ge(c_zero, 3)
                for e in range(2):
                    r = slice(e * L, (e + 1) * L)
                    ins = dve.tensor_tensor(kv_bd[r, :, e * L:(e + 1) * L], ctx3[0][r], ctx3[1][r],
                                            ALU.add)
                ins.then_inc(c_kv, 1)

            link(dve.memset(moments[:], 1.0))
            link(dve.memset(spread[:], 1.0))
            atanh_weights()
            ternary_weights()
            run(dve, slot, {0: rope})

        @block.gpsimd
        def _(pool):
            def slot(i, p):
                t = 2 * i + p
                n1, n2, n3, b1, b2, b3, q = t, t - 2, t - 4, t - 1, t - 3, t - 5, 1 - p
                if p == 0 and on(i - 1, BATCH):
                    since(pool, p_e1, 2 * i - 2)
                    pool.tensor_copy(kv_cur[:], kv_bd[:, i - 1, :]).then_inc(g_kv, 1)
                if on(b1):
                    since(pool, v_y1, b1)
                    pool.tensor_tensor(xb[:], x_sb[:, b1, :], bo_row[:], ALU.add).then_inc(g_xb, 1)
                if on(n1):
                    pool.wait_ge(v_mask, n1 + 1)
                    pool.tensor_tensor(heads(Ls[:]), heads(Ls[:]), over_heads(m8[:, :, 0:1]),
                                       ALU.subtract).then_inc(g_d1, 1)
                    pool.wait_ge(v_rec1, n1 + 1)
                    pool.tensor_tensor(heads(mask[:]), heads(mask[:]),
                                       over_heads(r1[:, 1, :].rearrange("p (h o) -> p h o", o=1)),
                                       ALU.mult).then_inc(g_mr, 1)
                    pool.wait_ge(g_mr, n1 + 1)
                    pool.wait_ge(a_exp1, n1 + 1)
                    pool.tensor_tensor(Ls[:], Ls[:], mask[:], ALU.mult).then_inc(g_P1, 1)
                if on(n3):
                    pool.wait_ge(v_h, n3 + 1)
                    since(pool, p_hT, n3)
                    pool.tensor_tensor(hg, hh, g3[:], ALU.mult).then_inc(g_hg, 1)
                if on(b1) or on(b2) or on(b3):
                    pool.wait_ge(v_var, t)
                    pool.tensor_tensor(rstd[:], spread[:], minus_half[:], ALU.pow
                                       ).then_inc(g_rstd, 1)
                if on(b2):
                    pool.wait_ge(v_x2, b2 + 1)
                    since(pool, p_xqT, b2)
                    pool.tensor_tensor(xg[:], x2[q][:].rearrange("p (o d) -> p o d", o=1)
                                       .to_broadcast([P, 2, D]), g12[:], ALU.mult).then_inc(g_xg, 1)
                    pool.wait_ge(v_ms, b2 + 1)
                    pool.tensor_tensor(sqx[:, 2:3], sqx[:, 1:2], minus_half[:, 0:1], ALU.pow
                                       ).then_inc(g_rx, 1)
                if on(n2):
                    pool.wait_ge(v_rec2, n2 + 1)
                    pool.tensor_tensor(heads(P2_even_odd[p]), heads(P2_even_odd[p]),
                                       over_heads(r2[:, 1, :].rearrange("p (h o) -> p h o", o=1)),
                                       ALU.mult).then_inc(g_P2, 1)

            pool.memset(lat_k[:], 0.0).then_inc(c_zero, 1)
            pool.memset(lat_v[:], 0.0).then_inc(c_zero, 1)
            pool.memset(kv_bd[:], 0.0).then_inc(c_zero, 1)
            pool.memset(ident[:], 0.0).then_inc(c_const, 1)
            pool.memset(ones[:], 1.0).then_inc(c_const, 1)
            pool.memset(minus_half[:], -0.5).then_inc(c_const, 1)
            pool.wait_ge(c_const, 3)
            pool.affine_select(out=ident[:], in_=ident[:], compare_op=ALU.not_equal, fill=1.0,
                               base=0, pattern=[[-1, P]], channel_multiplier=1).then_inc(c_ident, 1)

            def first_loads():
                pool.wait_ge(ld_x, 16 * 2)
                pool.wait_ge(ld_back, 16 * 3)

            def loaded():
                pool.wait_ge(c_kv, 1)
                pool.wait_ge(ld_g, 16 * 3)

            run(pool, slot, {0: first_loads, 1: loaded})


def rope_tables():
    inv_freq = (1.0 / (10000.0 ** (np.arange(0, DC, 2, dtype=np.float32) / np.float32(DC))
                       .astype(np.float32))).astype(np.float32)
    freqs = np.arange(L, dtype=np.float32)[:, None] * inv_freq[None, :]
    sin = np.repeat(np.sin(freqs.astype(np.float64)), 2, axis=-1).astype(np.float32)
    cos = np.repeat(np.cos(freqs.astype(np.float64)), 2, axis=-1).astype(np.float32)
    sin[:, :DC // 2] = -sin[:, :DC // 2]
    return np.ascontiguousarray(np.stack([np.tile(cos.T, (2, 1)), np.tile(sin.T, (2, 1))], axis=1))


def layouts(v):
    x = v["x"]
    ctx = v["ctx_512"].reshape(BATCH * L, DC).T
    rot = np.concatenate([ctx[DC // 2:], ctx[:DC // 2]])

    def chunked(w):
        return w.reshape(-1, P, w.shape[1]).transpose(1, 0, 2)

    lat = v["L0_attn_latent_keys"]
    return {
        "x": x.reshape(TILES, P, D).transpose(1, 0, 2),
        "xT": x.reshape(BATCH, SEQ, KD, P).transpose(3, 0, 2, 1),
        "wqT1": chunked(v["L0_attn_Wq"].T), "wvT1": chunked(v["L0_attn_Wv"].T),
        "woT1": chunked(v["L0_attn_Wo"].T),
        "bqv": np.stack([v["L0_attn_bq"].reshape(KD, P).T, v["L0_attn_bv"].reshape(KD, P).T], 1),
        "bo": v["L0_attn_bo"].reshape(1, D),
        "latT": chunked(lat.T), "lat": lat.reshape(L, PAIRS, 2, HD),
        "ctxT": np.tile(np.stack([ctx, rot], 1), (2, 1, 1)),
        "wkrT": v["L0_xattn_W_kr"].transpose(2, 0, 1), "wqrT": v["L0_xattn_W_qr"].transpose(2, 0, 1),
        "wkcqT": v["L0_xattn_w_kc_q"].transpose(2, 0, 1),
        "wqx": v["L0_xattn_Wq"].reshape(H, HK, D).transpose(1, 0, 2),
        "wkckv": v["L0_xattn_w_kc_kv"].transpose(1, 0, 2),
        "woTx": v["L0_xattn_Wo"].T.reshape(H, HK, D).transpose(1, 0, 2),
        "w1T": chunked(v["L0_ffn_w1"].T), "w2T": chunked(v["L0_ffn_w2"].T),
        "w3T": chunked(v["L0_ffn_w3"].T),
        "g1": v["L0_ffn_g1"].reshape(1, D), "g2": v["L0_ffn_g2"].reshape(1, D),
        "g3": v["L0_ffn_g3"].reshape(1, FF),
        "rope": rope_tables(),
    }


def kernel(**inputs):
    import concourse.bacc as bacc
    from concourse.bass_utils import run_bass_kernel_spmd

    nc = bacc.Bacc("TRN2", target_bir_lowering=False, num_devices=1)
    arrays, args = {}, {}
    for name, value in layouts({k: np.asarray(v) for k, v in inputs.items()}).items():
        value = np.ascontiguousarray(value)
        arrays[f"in_{name}"] = value
        args[name] = nc.dram_tensor(f"in_{name}", value.shape, mybir.dt.from_np(value.dtype),
                                    kind="ExternalInput").ap()
    out = nc.dram_tensor("out_x", (TILES, P, D), F32, kind="ExternalOutput").ap()
    decoder_layer(nc, args, out)
    r = run_bass_kernel_spmd(nc, [arrays], core_ids=[0])
    return r.results[0]["out_x"].reshape(BATCH, SEQ, D)
```

```python
from contextlib import ExitStack

import numpy as np

import concourse.bass as bass
from concourse import mybir

ALU = mybir.AluOpType
ACT = mybir.ActivationFunctionType
AX = mybir.AxisListType.X
F32 = mybir.dt.float32
F32R = mybir.dt.float32r
BF16 = mybir.dt.bfloat16

P = 128
D = 256
KD = D // P
BATCH, SEQ = 8, 256
TILES = BATCH * SEQ // P
H = 16
HD = D // H
L = 64
WIDE = H * L
PAIRS = H // 2
TOPK = 4
DC, RR, DCQ, HK = 64, 64, 192, 128
FF = 1024
FC = FF // P
LN_EPS, RMS_EPS, QUANT_MIN = 1e-5, 1e-8, 1e-4
ROUND = 12582912.0
QMAX = 127.0
HALF_ATANH = 0.5493061443340549
TAIL = TILES + 2
SLOTS = TILES + 5
PARTS = ((0, 0), (0, 1), (1, 0))
LOOP_FROM, LOOP_TO = 3, 7


def decoder_layer(nc, a, out):
    with ExitStack() as ctx:
        def sb(name, shape, dt=F32):
            return ctx.enter_context(nc.sbuf_tensor(name, shape, dt))

        def sems(*names):
            return [ctx.enter_context(nc.semaphore(n)) for n in names]

        x_sb = sb("x_sb", [P, TILES, D])
        xT = sb("xT", [P, BATCH, KD, SEQ])
        wqT1 = sb("wqT1", [P, KD, D])
        wvT1 = sb("wvT1", [P, KD, D])
        woT1 = sb("woT1", [P, KD, D])
        bqv = sb("bqv", [P, 2, KD])
        bo_row = sb("bo_row", [P, D])
        lat_k = sb("lat_k", [P, KD, 4 * L])
        lat_v = sb("lat_v", [P, PAIRS, 2 * HD])
        ident = sb("ident", [P, P])
        ones = sb("ones", [P, P])
        minus_half = sb("minus_half", [P, 4])
        kv_bd = sb("kv_bd", [P, BATCH, P])
        ctx_raw = sb("ctx_raw", [P, 2, BATCH * L])
        rope_sb = sb("rope_sb", [P, 2, L])
        kv_now = sb("kv_now", [P, P])
        kv_cur = sb("kv_cur", [P, 2, P], F32R)
        C_sb = sb("C_sb", [P, 2, PAIRS, D], F32R)
        wkckv = sb("wkckv", [P, H, DC])
        tern12 = sb("tern12", [P, 2, KD, FF], BF16)
        tern3 = sb("tern3", [P, FC, D], BF16)
        A_sb = sb("A_sb", [P, PAIRS, D])
        B_sb = sb("B_sb", [P, 2, KD, WIDE], F32R)
        x1T = sb("x1T", [P, 2, KD, P], F32R)
        w12_raw = [xT[:, BATCH // 2:BATCH], x_sb[:, 0:TILES // 2]]
        w3_raw = x_sb[:, TILES // 2:TILES]
        region_q = sb("region_q", [P, H * D])
        wqx = region_q[:, :].rearrange("p (h d) -> p h d", h=H)
        g3 = region_q[:, 0:FF]
        g12 = region_q[:, FF:FF + 2 * D].rearrange("p (w d) -> p w d", w=2)
        xg = region_q[:, FF + 2 * D:FF + 4 * D].rearrange("p (w d) -> p w d", w=2)
        x1, x2, x3 = ([region_q[:, FF + k * D:FF + (k + 1) * D] for k in ks]
                      for ks in ((4, 5), (6, 7, 8), (9, 10)))
        region_c = sb("region_c", [P, 2 * H * HK])
        wkcqT_a = region_c[:, 0:H * HK].rearrange("p (h k) -> p h k", h=H)
        wkcqT_b = region_c[0:DCQ - P, H * HK:2 * H * HK].rearrange("p (h k) -> p h k", h=H)
        woTx = region_c[:, :].rearrange("p (h d) -> p h d", h=H)
        th, hh, hg, junk_h = (region_c[:, k * FF:(k + 1) * FF] for k in range(4))
        region_r = sb("region_r", [P, H * DCQ])
        wqrT = region_r[0:RR, :].rearrange("p (h q) -> p h q", h=H)
        P2_even_odd = [region_r[:, 0:WIDE], region_r[:, 2 * WIDE:3 * WIDE]]
        PT2 = region_r[:, WIDE:2 * WIDE].rearrange("p (c t) -> p c t", c=PAIRS)
        region_t = sb("region_t", [P, 2 * WIDE])
        T1a, T1b = region_t[:, 0:WIDE], region_t[0:DCQ - P, WIDE:2 * WIDE]
        V_sb = region_t[:, :].rearrange("p (c n) -> p c n", c=PAIRS)
        region_u = sb("region_u", [P, 2 * WIDE])
        wkrT = region_u[0:RR, 0:WIDE].rearrange("p (h d) -> p h d", h=H)
        T2 = region_u[:, WIDE:2 * WIDE]
        PT1 = region_u[:, 0:WIDE].rearrange("p (c t) -> p c t", c=PAIRS)
        AT = region_u[:, WIDE:WIDE + D].rearrange("p (k t) -> p k t", k=KD)
        y = [region_u[:, WIDE + k * D:WIDE + (k + 1) * D] for k in (1, 2, 3)]
        QT = sb("QT", [P, KD, SEQ])
        Ls = sb("Ls", [P, WIDE])
        mask = sb("mask", [P, WIDE])
        m8 = sb("m8", [P, H, 8])
        d4 = sb("d4", [P, H, TOPK])
        r1 = sb("r1", [P, 2, H])
        xb = sb("xb", [P, D])
        m2 = sb("m2", [P, H])
        r2 = sb("r2", [P, 2, H])
        stats = sb("stats", [P, 3, 6])
        moments = sb("moments", [P, 3, 2])
        spread = sb("spread", [P, 4])
        rstd = sb("rstd", [P, 4])
        junk_x = sb("junk_x", [P, D])
        sqx = sb("sqx", [P, 4])
        amax = sb("amax", [P, 2])
        cq = sb("cq", [P, 2])
        icq = sb("icq", [P, 2])
        sq = sb("sq", [P, 2])
        dq = sb("dq", [P, 2])
        tq = sb("tq", [P, 2, 2])
        xqT = sb("xqT", [P, 2 * KD, P], BF16)
        sqh = sb("sqh", [P, 1])
        ch = sb("ch", [P, 4])
        dq3 = sb("dq3", [P, 2])
        hqT = sb("hqT", [P, FC, P], BF16)
        atanh_q = sb("atanh_q", [P, 3])
        prep = sb("prep", [P, 10, 3])

        wide = [ctx.enter_context(nc.psum_tensor(f"wide{k}", [P, WIDE], F32)) for k in range(3)]
        small = [ctx.enter_context(nc.psum_tensor(f"small{k}", [P, 512], F32)) for k in range(2)]

        ld_t, ld_t2, ld_s1, ld_back, ld_x, ld_ctx, ld_a, ld_c, ld_g, ld_raw, stored = sems(
            "ld_t", "ld_t2", "ld_s1", "ld_back", "ld_x", "ld_ctx", "ld_a", "ld_c", "ld_g",
            "ld_raw", "stored")
        ld_xT = sems(*[f"ld_xT{b}" for b in range(BATCH)])
        c_zero, c_ident, c_const, c_kv, c_chain, c_tern, c_mean = sems(
            "c_zero", "c_ident", "c_const", "c_kv", "c_chain", "c_tern", "c_mean")
        pre_mm, pre_ev, pre_abs, pre_sum, pre_ln, pre_lnin, pre_lo = sems(
            "pre_mm", "pre_ev", "pre_abs", "pre_sum", "pre_ln", "pre_lnin", "pre_lo")
        (p_QT, p_x1T, p_xqT, p_L1, p_L2, p_z1, p_z2, p_e0, p_e1, p_PT1, p_WT, p_hT, p_O1, p_PT2,
         p_O2, p_O3) = sems(*("p_QT p_x1T p_xqT p_L1 p_L2 p_z1 p_z2 p_e0 p_e1 p_PT1 p_WT p_hT p_O1 "
                              "p_PT2 p_O2 p_O3").split())
        (a_QT, a_x1T, a_xqT, a_L1, a_e4, a_tanh, a_exp1, a_exp2, a_sqh, a_e0, a_e1, a_sqx, a_PT1,
         a_AT, a_hT, a_PT2, a_quant) = sems(
             *("a_QT a_x1T a_xqT a_L1 a_e4 a_tanh a_exp1 a_exp2 a_sqh a_e0 a_e1 a_sqx a_PT1 "
               "a_AT a_hT a_PT2 a_quant").split())
        (v_y1, v_y2, v_y3, v_st1, v_st2, v_st3, v_mom, v_var, v_x1, v_x2, v_x3, v_max8, v_d4,
         v_mask, v_sum1, v_rec1, v_max2, v_sub2, v_sum2, v_rec2, v_u, v_h, v_amax, v_ms, v_cq,
         v_icq, v_sq, v_dq, v_tqh, v_tq, v_amaxh, v_msh, v_cqh, v_icqh, v_sqh, v_dqh,
         v_quanth, v_x1T, v_b0, v_b1) = sems(
             *("v_y1 v_y2 v_y3 v_st1 v_st2 v_st3 v_mom v_var v_x1 v_x2 v_x3 v_max8 v_d4 v_mask "
               "v_sum1 v_rec1 v_max2 v_sub2 v_sum2 v_rec2 v_u v_h v_amax v_ms v_cq v_icq v_sq v_dq "
               "v_tqh v_tq v_amaxh v_msh v_cqh v_icqh v_sqh v_dqh v_quanth v_x1T v_b0 v_b1"
               ).split())
        (g_rstd, g_xb, g_d1, g_mr, g_P1, g_kv, g_xg, g_rx, g_hg, g_P2) = sems(
            *"g_rstd g_xb g_d1 g_mr g_P1 g_kv g_xg g_rx g_hg g_P2".split())

        def since(eng, sem, count):
            if not isinstance(count, int) or count > 0:
                eng.wait_ge(sem, count)

        def on(n, total=TILES):
            return not isinstance(n, int) or 0 <= n < total

        def x2_of(n, parity):
            return x2[2 if isinstance(n, int) and n == TILES - 1 else parity]

        def in_tail(t, first=TAIL):
            return isinstance(t, int) and t >= first

        def upto(n, total=TILES):
            return min(n, total) if isinstance(n, int) else n

        def bank_free(eng, steady, *idle):
            for sem, count in (steady, *idle) if isinstance(steady[1], int) else (steady,):
                since(eng, sem, upto(count))

        def run(eng, slot, after={}):
            for t in range(2 * LOOP_FROM):
                slot(t // 2, t % 2)
                if t in after:
                    after[t]()
            with eng.Fori(LOOP_FROM, LOOP_TO) as i:
                slot(i, 0), slot(i, 1)
            for t in range(2 * LOOP_TO, SLOTS):
                slot(t // 2, t % 2)

        def roots_before(t):
            return TAIL - 1 + sum(on(u - 3) + on(u - 4) + on(u - 5) for u in range(TAIL, t))

        def heads(ap):
            return ap.rearrange("p (h l) -> p h l", h=H)

        def over_heads(column):
            return column.to_broadcast([P, H, L])

        block = ctx.enter_context(nc.Block())

        @block.sync
        def _(sp):
            sp.dma_start(wkrT, a["wkrT"]).then_inc(ld_t, 16)
            sp.dma_start(wqrT, a["wqrT"]).then_inc(ld_t, 16)
            sp.dma_start(wkcqT_a, a["wkcqT"][0:P]).then_inc(ld_t2, 16)
            sp.dma_start(wkcqT_b, a["wkcqT"][P:DCQ]).then_inc(ld_t2, 16)
            sp.dma_start(w12_raw[0].rearrange("p b k t -> p (b k t)"), a["w1T"]
                         ).then_inc(ld_raw, 16)
            sp.dma_start(w12_raw[1].rearrange("p t d -> p (t d)"), a["w2T"]).then_inc(ld_raw, 16)
            sp.dma_start(w3_raw, a["w3T"]).then_inc(ld_raw, 16)
            sp.dma_start(wqT1[:], a["wqT1"]).then_inc(ld_s1, 16)
            sp.dma_start(xT[:, 0], a["xT"][:, 0]).then_inc(ld_xT[0], 16)
            sp.dma_start(bqv[:], a["bqv"]).then_inc(ld_s1, 16)
            sp.wait_ge(c_zero, 2)
            for q in range(P // HD):
                sp.dma_start(lat_k[HD * q:HD * (q + 1), :, L * (q % 4):L * (q % 4 + 1)],
                             a["latT"][HD * q:HD * (q + 1)]).then_inc(ld_s1, 16)
            for e in range(2):
                sp.dma_start(lat_v[L * e:L * (e + 1), :, HD * e:HD * (e + 1)],
                             a["lat"][:, :, e]).then_inc(ld_s1, 16)
            sp.dma_start(wqx, a["wqx"]).then_inc(ld_a, 16)
            sp.dma_start(ctx_raw[:], a["ctxT"]).then_inc(ld_ctx, 16)
            sp.dma_start(rope_sb[:], a["rope"]).then_inc(ld_ctx, 16)
            sp.dma_start(wvT1[:], a["wvT1"]).then_inc(ld_back, 16)
            sp.dma_start(woT1[:], a["woT1"]).then_inc(ld_back, 16)
            sp.dma_start(bo_row[:], a["bo"].to_broadcast([P, D])).then_inc(ld_back, 16)
            sp.dma_start(xT[:, 1], a["xT"][:, 1]).then_inc(ld_xT[1], 16)
            sp.dma_start(wkckv[:], a["wkckv"]).then_inc(ld_c, 16)
            sp.wait_ge(pre_mm, 3)
            sp.dma_start(woTx, a["woTx"]).then_inc(ld_c, 16)
            sp.wait_ge(c_tern, 3)
            sp.dma_start(x_sb[:, 0:2], a["x"][:, 0:2]).then_inc(ld_x, 16)
            sp.dma_start(x_sb[:, 2:TILES], a["x"][:, 2:TILES]).then_inc(ld_x, 16)
            for b in range(2, BATCH):
                sp.dma_start(xT[:, b], a["xT"][:, b]).then_inc(ld_xT[b], 16)
            sp.wait_ge(pre_mm, 4)
            for k, name in enumerate(("g1", "g2")):
                sp.dma_start(g12[:, k, :], a[name].to_broadcast([P, D])).then_inc(ld_g, 16)
            sp.dma_start(g3, a["g3"].to_broadcast([P, FF])).then_inc(ld_g, 16)

            def slot(i, p):
                b3 = 2 * i + p - 5
                if on(b3):
                    sp.wait_ge(v_x3, b3 + 1)
                    sp.dma_start(out[b3], x3[1 - p]).then_inc(stored, 16)

            run(sp, slot)
            sp.wait_ge(stored, 16 * TILES)

        @block.tensor
        def _(pe):
            def project_q(b):
                for g in range(KD):
                    for k in range(KD):
                        mm = pe.matmul(small[1][:, g * SEQ:(g + 1) * SEQ],
                                       wqT1[:, k, g * P:(g + 1) * P], xT[:, b, k, :],
                                       start=(k == 0), stop=(k == KD - 1))
                mm.then_inc(p_QT, 1)

            def slot(i, p):
                t = 2 * i + p
                n1, n2, n3, b1, b2, b3, q = t, t - 2, t - 4, t - 1, t - 3, t - 5, 1 - p
                tail = in_tail(t)

                def turn_h():
                    if on(b3):
                        pe.wait_ge(v_quanth, b3 + 1)
                        if tail:
                            bank_free(pe, (v_u, n3 + 1), (a_hT, b3))
                        elif p == 0:
                            bank_free(pe, (v_b1, upto(i, BATCH)), (v_u, n3), (a_hT, b3))
                        else:
                            bank_free(pe, (a_e1, upto(t - 1, 2 * BATCH)), (v_u, n3), (a_hT, b3))
                        for c in range(FC):
                            mm = pe.transpose(wide[2][:, c * P:(c + 1) * P],
                                              hg[:, c * P:(c + 1) * P], ident[:])
                        mm.then_inc(p_hT, 1)

                def output_3():
                    if on(b3):
                        pe.wait_ge(a_hT, b3 + 1)
                        if tail:
                            bank_free(pe, (v_y2, b2 + 1), (v_y3, b3))
                        else:
                            bank_free(pe, (a_AT, b1 + 1), (v_y2, b2), (v_y3, b3))
                        for c in range(FC):
                            mm = pe.matmul(small[0][:, 0:D], hqT[:, c, :], tern3[:, c, :],
                                           start=(c == 0), stop=(c == FC - 1))
                        mm.then_inc(p_O3, 1)

                def turn_x2():
                    if on(n3):
                        pe.wait_ge(a_quant, n3 + 1)
                        bank_free(pe, (v_y1, b1 + 1), (v_x1T, n2 + 1), (a_xqT, n3),
                                  (a_QT, upto(i + 1, BATCH)))
                        for k in range(2 * KD):
                            mm = pe.transpose(small[1][:, k * P:(k + 1) * P],
                                              xg[:, k // KD, (k % KD) * P:(k % KD + 1) * P],
                                              ident[:])
                        mm.then_inc(p_xqT, 1)

                def turn_P2():
                    if on(b2):
                        pe.wait_ge(g_P2, b2 + 1)
                        bank_free(pe, (a_L1, n1 + 1), (a_e0, upto(t - 1, 2 * BATCH)),
                                  (v_b0, upto(i, BATCH)), (a_PT2, b2))
                        for c in range(PAIRS):
                            mm = pe.transpose(wide[1][:, c * P:(c + 1) * P],
                                              P2_even_odd[q][:, c * P:(c + 1) * P],
                                              ident[:])
                        mm.then_inc(p_PT2, 1)

                def hidden():
                    if on(n3):
                        pe.wait_ge(a_xqT, n3 + 1)
                        bank_free(pe, (a_hT, b3 if tail else b3 + 1),
                                  (a_e1, upto(t - 1, 2 * BATCH)), (v_b1, upto(i, BATCH)), (v_u, n3))
                        for w, sem in enumerate((p_z1, p_z2)):
                            if w == 1:
                                bank_free(pe, (v_sub2, n2 + 1), (a_PT1, b1 + 1), (v_h, n3))
                            for r in range(2):
                                for k in range(KD):
                                    mm = pe.matmul(wide[2 - 2 * w][:, r * 512:(r + 1) * 512],
                                                   xqT[:, w * KD + k, :],
                                                   tern12[:, w, k, r * 512:(r + 1) * 512],
                                                   start=(k == 0), stop=(k == KD - 1))
                            mm.then_inc(sem, 1)

                def output_2():
                    if on(b2):
                        pe.wait_ge(a_PT2, b2 + 1)
                        pe.wait_ge(a_e1, 2 * (i - q))
                        bank_free(pe, (v_y3, b3 if tail else b3 + 1), (a_AT, b1 + 1), (v_y2, b2))
                        for c in range(PAIRS):
                            mm = pe.matmul(small[0][:, 0:D], PT2[:, c, :], V_sb[:, c, :],
                                           start=(c == 0), stop=(c == PAIRS - 1))
                        mm.then_inc(p_O2, 1)

                if isinstance(i, int) and p == 0 and i < BATCH:
                    pe.wait_ge(ld_xT[i], 16)
                if on(b1):
                    bank_free(pe, (v_y2, b2), (v_y3, b3), (a_AT, b1))
                    for g in range(KD):
                        for k in range(KD):
                            pe.matmul(small[0][:, g * P:(g + 1) * P], wvT1[:, k, g * P:(g + 1) * P],
                                      xT[:, i - q, k, q * P:(q + 1) * P],
                                      start=(g == 0 and k == 0), stop=False, skip_group_check=True)
                    pe.wait_ge(g_P1, b1 + 1)
                    bank_free(pe, (v_h, b3 + 1), (v_sub2, n2), (a_PT1, b1))
                    for c in range(PAIRS):
                        mm = pe.transpose(wide[0][:, c * P:(c + 1) * P], Ls[:, c * P:(c + 1) * P],
                                          ident[:])
                    mm.then_inc(p_PT1, 1)
                if on(n1):
                    pe.wait_ge(a_QT, i + 1)
                    if p == 0:
                        bank_free(pe, (v_b0, i), (a_PT2, b2), (a_L1, n1))
                    else:
                        bank_free(pe, (a_e0, upto(t - 1, 2 * BATCH)), (v_b0, upto(i, BATCH)),
                                  (a_PT2, b2), (a_L1, n1))
                    for g in range(KD):
                        for j in range(2):
                            mm = pe.matmul(wide[1][:, j * 512 + g * SEQ:j * 512 + (g + 1) * SEQ],
                                           QT[j * L:(j + 1) * L, g, p * P:(p + 1) * P],
                                           lat_k[j * L:(j + 1) * L, g, :], start=True, stop=True)
                    mm.then_inc(p_L1, 1)
                if on(n2):
                    pe.wait_ge(v_x1, n2 + 1)
                    if p == 0:
                        bank_free(pe, (a_QT, upto(i + 1, BATCH)), (a_xqT, n3), (v_y1, b1))
                    else:
                        bank_free(pe, (a_xqT, n3), (v_y1, b1), (a_QT, upto(i + 1, BATCH)))
                    for k in range(KD):
                        mm = pe.transpose(small[1][:, k * P:(k + 1) * P],
                                          x1[p][:, k * P:(k + 1) * P], ident[:])
                    mm.then_inc(p_x1T, 1)
                if on(b1):
                    pe.wait_ge(a_PT1, b1 + 1)
                    for c in range(PAIRS):
                        g, r = divmod(c, PAIRS // KD)
                        mm = pe.matmul(small[0][32 * r:32 * (r + 1), g * P:(g + 1) * P],
                                       lat_v[:, c, :], PT1[:, c, :],
                                       start=False, stop=(c == PAIRS - 1), skip_group_check=True)
                    mm.then_inc(p_WT, 1)
                if tail:
                    turn_P2(), output_2(), turn_x2(), hidden(), turn_h(), output_3()
                else:
                    turn_h()
                    if on(n2):
                        pe.wait_ge(a_x1T, n2 + 1)
                        pe.wait_ge(v_b1, i)
                        bank_free(pe, (a_PT1, b1 + 1), (v_h, n3), (v_sub2, n2))
                        for u, w in PARTS:
                            if u == 1:
                                pe.wait_ge(v_x1T, n2 + 1)
                            for k in range(KD):
                                for r in range(2):
                                    mm = pe.matmul(wide[0][:, r * 512:(r + 1) * 512],
                                                   x1T[:, u, k, :],
                                                   B_sb[:, w, k, r * 512:(r + 1) * 512],
                                                   start=(u == w == k == 0),
                                                   stop=(u == 1 and k == KD - 1))
                        mm.then_inc(p_L2, 1)
                    if on(b1):
                        pe.wait_ge(a_AT, b1 + 1)
                        bank_free(pe, (v_x1T, n2 + 1), (a_xqT, n3), (v_y1, b1),
                                  (a_QT, upto(i + 1, BATCH)))
                        for g in range(KD):
                            mm = pe.matmul(small[1][:, 0:D], AT[:, g, :], woT1[:, g, :],
                                           start=(g == 0), stop=(g == KD - 1))
                        mm.then_inc(p_O1, 1)
                    output_3(), turn_x2(), turn_P2(), hidden(), output_2()
                if p == 1 and on(i + 1, BATCH):
                    if isinstance(i, int):
                        pe.wait_ge(ld_xT[i + 1], 16)
                    bank_free(pe, (a_xqT, n3 + 1), (v_y1, b1 + 1), (v_x1T, n2 + 1),
                              (a_QT, i + 1))
                    project_q(i + 1)
                if p == 0 and on(i - 1, BATCH):
                    pe.wait_ge(g_kv, 3 * i)
                    bank_free(pe, (a_PT2, b2 + 1), (a_L1, n1 + 1), (a_e0, t - 1), (v_b0, i))
                    bank_free(pe, (v_u, n3 + 1), (a_hT, b3 + 1), (a_e1, t - 1), (v_b1, i))
                    for half, sem in enumerate((p_e0, p_e1)):
                        for c in range(PAIRS // 2):
                            for u, w in PARTS:
                                mm = pe.matmul(wide[1 + half][:, c * D:(c + 1) * D],
                                               kv_cur[:, u, :],
                                               C_sb[:, w, half * PAIRS // 2 + c, :],
                                               start=(u == w == 0), stop=(u == 1))
                        mm.then_inc(sem, 1)
                if p == 1 and on(i, BATCH):
                    bank_free(pe, (a_PT2, b2 + 1), (a_L1, n1 + 1), (a_e0, t - 1), (v_b0, i))
                    bank_free(pe, (v_u, n3 + 1), (a_hT, b3 + 1), (a_e1, t - 1), (v_b1, i))
                    for k, sem in enumerate((p_e0, p_e1)):
                        for c in range(PAIRS):
                            mm = pe.matmul(wide[1 + k][:, c * P:(c + 1) * P],
                                           A_sb[:, c, k * P:(k + 1) * P], kv_bd[:, i, :],
                                           start=True, stop=True)
                        mm.then_inc(sem, 1)

            def side_weights():
                pe.wait_ge(ld_t, 16 * 2)
                for half, (lo, hi) in enumerate(((0, P), (P, DCQ))):
                    for h in range(H):
                        mm = pe.matmul(wide[1 + half][0:hi - lo, h * DC:(h + 1) * DC],
                                       wqrT[:, h, lo:hi], wkrT[:, h, :], start=True, stop=True)
                    mm.then_inc(pre_mm, 1)
                pe.wait_ge(ld_t2, 16 * 2)
                pe.wait_ge(pre_ev, 2)
                for h in range(H):
                    if h == H // 2:
                        ffn_sums()
                    pe.matmul(wide[0][:, h * DC:(h + 1) * DC], wkcqT_a[:, h, :],
                              T1a[:, h * DC:(h + 1) * DC], start=True, stop=False)
                    mm = pe.matmul(wide[0][:, h * DC:(h + 1) * DC], wkcqT_b[:, h, :],
                                   T1b[:, h * DC:(h + 1) * DC], start=False, stop=True)
                mm.then_inc(pre_mm, 1)

            def score_weights():
                pe.wait_ge(ld_a, 16)
                pe.wait_ge(a_L1, 1)
                pe.wait_ge(pre_ev, 3)
                for h in range(H):
                    c, e = divmod(h, 2)
                    mm = pe.matmul(wide[1 + c // 4][DC * e:DC * (e + 1),
                                                    (c % 4) * D:(c % 4 + 1) * D],
                                   T2[:, h * DC:(h + 1) * DC], wqx[:, h, :], start=True, stop=True)
                mm.then_inc(pre_mm, 1)
                pe.wait_ge(pre_ev, 5)
                pe.wait_ge(c_mean, 1)
                pe.wait_ge(c_kv, 2)

            def output_weights():
                pe.wait_ge(ld_c, 16 * 2)
                for half in range(2):
                    pe.wait_ge(pre_ev, 3 + half)
                    for h in range(half * H // 2, (half + 1) * H // 2):
                        c, e = divmod(h, 2)
                        mm = pe.matmul(wide[half][DC * e:DC * (e + 1), (c % 4) * D:(c % 4 + 1) * D],
                                       wkckv[:, h, :], woTx[:, h, :], start=True, stop=True)
                    mm.then_inc(pre_mm, 1)
                pe.wait_ge(pre_lo, 2)

            def ffn_sums():
                pe.wait_ge(c_const, 3)
                pe.wait_ge(pre_abs, 3)
                pe.matmul(small[0][:, 0:3], ones[:], prep[:, 0, :], start=True, stop=True
                          ).then_inc(pre_sum, 1)

            def first_weights():
                score_weights()
                output_weights()
                pe.wait_ge(ld_back, 16 * 3)
                pe.wait_ge(c_ident, 1)

            def loop_loads():
                pe.wait_ge(c_tern, 3)
                for b in range(LOOP_FROM, LOOP_TO + 1):
                    pe.wait_ge(ld_xT[b], 16)

            side_weights()
            pe.wait_ge(ld_s1, 16 * 12)
            pe.wait_ge(ld_xT[0], 16)
            project_q(0)
            run(pe, slot, {0: first_weights, 3: loop_loads})

        @block.scalar
        def _(act):
            def copy_q(b):
                act.wait_ge(p_QT, b + 1)
                for g in range(KD):
                    ins = act.activation(QT[:, g, :], small[1][:, g * SEQ:(g + 1) * SEQ],
                                         ACT.Identity, bias=bqv[:, 0, g:g + 1])
                ins.then_inc(a_QT, 1)

            def slot(i, p):
                t = 2 * i + p
                n1, n2, n3, b1, b2, b3, q = t, t - 2, t - 4, t - 1, t - 3, t - 5, 1 - p

                def copy_hT():
                    if on(b3):
                        act.wait_ge(p_hT, b3 + 1)
                        since(act, p_O3, b3)
                        act.activation(hqT[:], wide[2][:].rearrange("p (c t) -> p c t", c=FC),
                                       ACT.Copy, bias=-ROUND).then_inc(a_hT, 1)

                def whole_x2():
                    if on(n3):
                        act.wait_ge(v_sq, n3 + 1)
                        for k in range(2):
                            ins = act.activation(xg[:, k, :], xg[:, k, :], ACT.Copy, bias=ROUND,
                                                 scale=sq[:, k:k + 1])
                        ins.then_inc(a_quant, 1)

                def copy_x2T():
                    if on(n3):
                        act.wait_ge(p_xqT, n3 + 1)
                        since(act, p_z2, n3)
                        act.activation(xqT[:], small[1][:].rearrange("p (k t) -> p k t", k=2 * KD),
                                       ACT.Copy, bias=-ROUND).then_inc(a_xqT, 1)

                def copy_P2T():
                    if on(b2):
                        act.wait_ge(p_PT2, b2 + 1)
                        since(act, p_O2, b2)
                        act.activation(PT2, wide[1][:].rearrange("p (c t) -> p c t", c=PAIRS),
                                       ACT.Copy).then_inc(a_PT2, 1)

                def tanh():
                    if on(n3):
                        act.wait_ge(p_z1, n3 + 1)
                        act.wait_ge(v_tq, n3 + 1)
                        since(act, v_h, n3)
                        act.activation(th, wide[2][:], ACT.Tanh, scale=tq[:, p, 0:1]
                                       ).then_inc(a_tanh, 1)

                def exp_2():
                    if on(n2):
                        act.wait_ge(v_sub2, n2 + 1)
                        act.activation(P2_even_odd[p], P2_even_odd[p], ACT.Exp
                                       ).then_inc(a_exp2, 1)

                def square_h():
                    if on(n3):
                        act.wait_ge(v_h, n3 + 1)
                        since(act, a_sqh, n3)
                        act.activation(junk_h, hh, ACT.Square, accum_out=sqh[:]
                                       ).then_inc(a_sqh, 1)

                def square_x2(n, parity):
                    if on(n):
                        act.wait_ge(v_x2, n + 1)
                        since(act, a_sqx, n)
                        act.activation(junk_x[:], x2_of(n, parity), ACT.Square,
                                       accum_out=sqx[:, 0:1]).then_inc(a_sqx, 1)

                if on(b1):
                    act.wait_ge(p_PT1, b1 + 1)
                    since(act, p_WT, b1)
                    act.activation(PT1, wide[0][:].rearrange("p (c t) -> p c t", c=PAIRS),
                                   ACT.Copy).then_inc(a_PT1, 1)
                if on(n1):
                    act.wait_ge(p_L1, n1 + 1)
                    since(act, p_PT1, n1)
                    for j in range(2):
                        ins = act.activation(
                            Ls[:].rearrange("p (g j n) -> p j g n", g=KD, j=2)[:, j],
                            wide[1][:, j * 512:(j + 1) * 512].rearrange("p (g n) -> p g n", g=KD),
                            ACT.Copy)
                    ins.then_inc(a_L1, 1)
                if on(n2):
                    act.wait_ge(p_x1T, n2 + 1)
                    since(act, p_L2, n2)
                    act.activation(x1T[:, 0], small[1][:, 0:D].rearrange("p (k t) -> p k t", k=KD),
                                   ACT.Copy).then_inc(a_x1T, 1)
                if on(b1):
                    act.wait_ge(p_WT, b1 + 1)
                    since(act, p_O1, b1)
                    for g in range(KD):
                        ins = act.activation(AT[:, g, :], small[0][:, g * P:(g + 1) * P],
                                             ACT.Identity, bias=bqv[:, 1, g:g + 1])
                    ins.then_inc(a_AT, 1)
                if in_tail(t):
                    copy_P2T()
                    if t == TAIL:
                        square_x2(b2 - 1, p)
                    whole_x2(), copy_x2T(), square_x2(b2, q), tanh(), square_h(), copy_hT()
                    return
                copy_hT(), whole_x2()
                if on(n1):
                    act.wait_ge(v_d4, n1 + 1)
                    act.activation(d4[:], d4[:], ACT.Exp, scale=HD ** -0.5).then_inc(a_e4, 1)
                copy_x2T()
                copy_P2T()
                if in_tail(t, TAIL - 1):
                    exp_2(), tanh()
                else:
                    tanh()
                    if on(n1):
                        act.wait_ge(g_d1, n1 + 1)
                        act.activation(Ls[:], Ls[:], ACT.Exp, scale=HD ** -0.5).then_inc(a_exp1, 1)
                    exp_2()
                square_h()
                if p == 1 and on(i + 1, BATCH):
                    copy_q(i + 1)
                copy_spare(i, p, 0)
                copy_spare(i, p, 1)
                if not in_tail(t, TAIL - 1):
                    square_x2(b2, q)

            def copy_spare(i, p, half):
                ready, copied = ((p_e0, a_e0), (p_e1, a_e1))[half]
                if p == 0 and on(i - 1, BATCH):
                    act.wait_ge(ready, 2 * i)
                    since(act, p_O2, 2 * i - 3)
                    act.activation(V_sb[:, half * 4:(half + 1) * 4, :],
                                   wide[1 + half][:].rearrange("p (c n) -> p c n", c=4),
                                   ACT.Copy).then_inc(copied, 1)
                if p == 1 and on(i, BATCH):
                    act.wait_ge(ready, 2 * i + 1)
                    act.activation(B_sb[:, 0, half, :], wide[1 + half][:], ACT.Copy
                                   ).then_inc(copied, 1)

            def side_weights():
                act.wait_ge(pre_mm, 1)
                act.activation(T1a, wide[1][:], ACT.Copy).then_inc(pre_ev, 1)
                act.wait_ge(pre_mm, 2)
                act.activation(T1b, wide[2][0:DCQ - P, :], ACT.Copy).then_inc(pre_ev, 1)
                ffn_sums()
                act.wait_ge(pre_mm, 3)
                act.activation(T2, wide[0][:], ACT.Copy).then_inc(pre_ev, 1)

            def score_weights():
                act.wait_ge(pre_mm, 4)
                for half in range(2):
                    act.activation(A_sb[:, 4 * half:4 * half + 4, :],
                                   wide[1 + half][:].rearrange("p (c n) -> p c n", c=4),
                                   ACT.Copy).then_inc(pre_ev, 1)

            def output_weights():
                for half in range(2):
                    act.wait_ge(pre_mm, 5 + half)
                    act.activation(C_sb[:, 0, 4 * half:4 * half + 4, :],
                                   wide[half][:].rearrange("p (c n) -> p c n", c=4),
                                   ACT.Copy).then_inc(pre_ev, 1)
                act.wait_ge(c_tern, 3)

            def ffn_sums():
                act.wait_ge(ld_raw, 16 * 3)
                for w in range(2):
                    act.activation(tern12[:, w].rearrange("p k f -> p (k f)"),
                                   w12_raw[w].rearrange(
                                       ("p b k t -> p (b k t)", "p t d -> p (t d)")[w]), ACT.Abs,
                                   accum_out=prep[:, 0, w:w + 1]).then_inc(pre_abs, 1)
                act.activation(tern3[:].rearrange("p c d -> p (c d)"),
                               w3_raw.rearrange("p c d -> p (c d)"), ACT.Abs,
                               accum_out=prep[:, 0, 2:3]).then_inc(pre_abs, 1)
                act.wait_ge(pre_lnin, 1)
                act.activation(prep[:, 5, :], prep[:, 4, :], ACT.Ln).then_inc(pre_ln, 1)

            def first_weights():
                score_weights()
                output_weights()

            side_weights()
            act.wait_ge(ld_s1, 16 * 12)
            copy_q(0)
            run(act, slot, {0: first_weights})

        @block.vector
        def _(dve):
            def moments_of(k, n, sem_y, sem_st):
                dve.wait_ge(sem_y, n + 1)
                dve.bn_stats(stats[:, k, :], y[k]).then_inc(sem_st, 1)
                dve.wait_ge(c_zero, 3)
                dve.wait_ge(sem_st, n + 1)
                dve.bn_aggr(moments[:, k, :], stats[:, k, :]).then_inc(v_mom, 1)

            def slot(i, p):
                t = 2 * i + p
                n1, n2, n3, b1, b2, b3, q = t, t - 2, t - 4, t - 1, t - 3, t - 5, 1 - p

                def residual_3():
                    if on(b3):
                        dve.wait_ge(p_O3, b3 + 1)
                        dve.wait_ge(v_dqh, b3 + 1)
                        since(dve, v_x3, b3)
                        dve.scalar_tensor_tensor(y[2], small[0][:, 0:D], dq3[:, q:q + 1],
                                                 x2_of(b3, q), ALU.mult, ALU.add).then_inc(v_y3, 1)

                def gate():
                    if on(n3):
                        dve.wait_ge(a_tanh, n3 + 1)
                        dve.scalar_tensor_tensor(th, th, 1.0, wide[2][:], ALU.add, ALU.mult
                                                 ).then_inc(v_u, 1)
                        dve.wait_ge(v_u, n3 + 1)
                        dve.wait_ge(p_z2, n3 + 1)
                        since(dve, a_sqh, n3)
                        since(dve, g_hg, n3)
                        dve.scalar_tensor_tensor(hh, wide[0][:], tq[:, p, 1:2], th, ALU.mult,
                                                 ALU.mult).then_inc(v_h, 1)

                def sums_2():
                    if on(n2):
                        dve.wait_ge(a_exp2, n2 + 1)
                        dve.tensor_reduce(r2[:, 0, :], heads(P2_even_odd[p]), AX, ALU.add
                                          ).then_inc(v_sum2, 1)
                        dve.wait_ge(v_sum2, n2 + 1)
                        dve.reciprocal(r2[:, 1, :], r2[:, 0, :]).then_inc(v_rec2, 1)

                def mean_square_h():
                    if on(n3):
                        dve.wait_ge(a_sqh, n3 + 1)
                        dve.tensor_scalar(spread[:, 3:4], sqh[:], 1.0 / FF, RMS_EPS, ALU.mult,
                                          ALU.add).then_inc(v_msh, 1)

                def residual_2():
                    if on(b2):
                        dve.wait_ge(p_O2, b2 + 1)
                        since(dve, v_x2, b2)
                        dve.tensor_tensor(y[1], small[0][:, 0:D], x1[q], ALU.add).then_inc(v_y2, 1)
                        moments_of(1, b2, v_y2, v_st2)

                def largest_h():
                    if on(n3):
                        dve.wait_ge(g_hg, n3 + 1)
                        dve.tensor_reduce(ch[:, 0:1], hg, AX, ALU.max, apply_absolute_value=True
                                          ).then_inc(v_amaxh, 1)

                def scale_h():
                    if on(n3):
                        dve.wait_ge(v_amaxh, n3 + 1)
                        dve.tensor_scalar(ch[:, 1:2], ch[:, 0:1], rstd[:, 3:4], QUANT_MIN, ALU.mult,
                                          ALU.max).then_inc(v_cqh, 1)
                        dve.wait_ge(v_cqh, n3 + 1)
                        dve.reciprocal(ch[:, 2:3], ch[:, 1:2]).then_inc(v_icqh, 1)
                        dve.tensor_tensor(dq3[:, p:p + 1], ch[:, 1:2], atanh_q[:, 2:3], ALU.mult
                                          ).then_inc(v_dqh, 1)
                        dve.wait_ge(v_icqh, n3 + 1)
                        dve.tensor_scalar(ch[:, 3:4], ch[:, 2:3], rstd[:, 3:4], QMAX, ALU.mult,
                                          ALU.mult).then_inc(v_sqh, 1)
                        dve.wait_ge(v_sqh, n3 + 1)
                        dve.tensor_scalar(hg, hg, ch[:, 3:4], ROUND, ALU.mult, ALU.add
                                          ).then_inc(v_quanth, 1)

                def scale_x2():
                    if on(b2):
                        dve.wait_ge(a_sqx, b2 + 1)
                        dve.tensor_scalar(sqx[:, 1:2], sqx[:, 0:1], 1.0 / D, RMS_EPS, ALU.mult,
                                          ALU.add).then_inc(v_ms, 1)
                        dve.wait_ge(g_xg, b2 + 1)
                        dve.tensor_reduce(amax[:], xg, AX, ALU.max, apply_absolute_value=True
                                          ).then_inc(v_amax, 1)
                        dve.wait_ge(v_amax, b2 + 1)
                        dve.wait_ge(g_rx, b2 + 1)
                        dve.tensor_scalar(cq[:], amax[:], sqx[:, 2:3], QUANT_MIN, ALU.mult, ALU.max
                                          ).then_inc(v_cq, 1)
                        dve.wait_ge(v_cq, b2 + 1)
                        dve.reciprocal(icq[:], cq[:]).then_inc(v_icq, 1)
                        dve.tensor_tensor(dq[:], cq[:], atanh_q[:, 0:2], ALU.mult).then_inc(v_dq, 1)
                        dve.wait_ge(v_icq, b2 + 1)
                        dve.tensor_scalar(sq[:], icq[:], sqx[:, 2:3], QMAX, ALU.mult, ALU.mult
                                          ).then_inc(v_sq, 1)
                        dve.wait_ge(v_dq, b2 + 1)
                        dve.tensor_scalar(tq[:, q, 0:1], dq[:, 0:1], 0.5, None, ALU.mult
                                          ).then_inc(v_tqh, 1)
                        dve.wait_ge(v_tqh, b2 + 1)
                        dve.tensor_tensor(tq[:, q, 1:2], tq[:, q, 0:1], dq[:, 1:2], ALU.mult
                                          ).then_inc(v_tq, 1)

                def layernorm_in_tail(k, n, dst, sem, moments_made, rounds):
                    dve.wait_ge(v_mom, moments_made)
                    dve.tensor_scalar(spread[:, 0:3], moments[:, :, 1], LN_EPS, None, ALU.add
                                      ).then_inc(v_var, 1)
                    dve.wait_ge(g_rstd, rounds)
                    if k == 2:
                        since(dve, stored, 16 * n)
                    dve.tensor_scalar(dst, y[k], moments[:, k, 0:1], rstd[:, k:k + 1],
                                      ALU.subtract, ALU.mult).then_inc(sem, 1)

                if in_tail(t):
                    made = TILES + upto(b2 + 1) + b3
                    rounds = roots_before(t)
                    if on(b2):
                        residual_2()
                        rounds += 1
                        layernorm_in_tail(1, b2, x2_of(b2, q), v_x2, made, rounds)
                        scale_x2()
                    if on(n3):
                        gate(), mean_square_h(), largest_h()
                        rounds += 1
                        dve.wait_ge(g_rstd, rounds)
                        scale_h()
                    residual_3()
                    moments_of(2, b3, v_y3, v_st3)
                    layernorm_in_tail(2, b3, x3[q], v_x3, made + 1, rounds + 1)
                    return

                if on(n1):
                    dve.wait_ge(a_L1, n1 + 1)
                    since(dve, g_d1, n1)
                if on(n2):
                    dve.wait_ge(a_x1T, n2 + 1)
                    dve.tensor_tensor(x1T[:, 1],
                                      small[1][:, 0:D].rearrange("p (k t) -> p k t", k=KD),
                                      x1T[:, 0], ALU.subtract).then_inc(v_x1T, 1)
                if on(n1):
                    for h in range(H):
                        ins = dve.max(m8[:, h, :], Ls[:, h * L:(h + 1) * L])
                    ins.then_inc(v_max8, 1)
                    dve.wait_ge(v_max8, n1 + 1)
                    dve.tensor_tensor(d4[:], m8[:, :, 0:TOPK],
                                      m8[:, :, 0:1].to_broadcast([P, H, TOPK]), ALU.subtract
                                      ).then_inc(v_d4, 1)
                    since(dve, g_P1, n1)
                    dve.tensor_tensor(heads(mask[:]), heads(Ls[:]),
                                      over_heads(m8[:, :, TOPK - 1:TOPK]), ALU.is_ge
                                      ).then_inc(v_mask, 1)
                if on(b1):
                    dve.wait_ge(p_O1, b1 + 1)
                    dve.wait_ge(g_xb, b1 + 1)
                    since(dve, v_x1, b1)
                    dve.tensor_tensor(y[0], small[1][:, 0:D], xb[:], ALU.add).then_inc(v_y1, 1)
                if on(n2):
                    dve.wait_ge(p_L2, n2 + 1)
                    dve.tensor_reduce(m2[:], heads(wide[0][:]), AX, ALU.max).then_inc(v_max2, 1)
                    dve.wait_ge(v_max2, n2 + 1)
                    since(dve, p_PT2, n2 - 1)
                    dve.tensor_tensor(heads(P2_even_odd[p]), heads(wide[0][:]),
                                      over_heads(m2[:].rearrange("p (h o) -> p h o", o=1)),
                                      ALU.subtract).then_inc(v_sub2, 1)
                if on(n1):
                    dve.wait_ge(a_e4, n1 + 1)
                    dve.tensor_reduce(r1[:, 0, :], d4[:], AX, ALU.add).then_inc(v_sum1, 1)
                    dve.wait_ge(v_sum1, n1 + 1)
                    since(dve, g_mr, n1)
                    dve.reciprocal(r1[:, 1, :], r1[:, 0, :]).then_inc(v_rec1, 1)
                residual_3()
                if on(b1):
                    moments_of(0, b1, v_y1, v_st1)
                if on(b3):
                    moments_of(2, b3, v_y3, v_st3)
                if in_tail(t, TAIL - 1):
                    sums_2(), gate()
                else:
                    gate(), sums_2()
                mean_square_h(), residual_2()
                if on(b1) or on(b2) or on(b3):
                    made = sum(max(0, upto(n + 1)) for n in (b1, b2, b3)) \
                        if isinstance(t, int) else 3 * t - 6
                    dve.wait_ge(v_mom, made)
                    dve.tensor_scalar(spread[:, 0:3], moments[:, :, 1], LN_EPS, None, ALU.add
                                      ).then_inc(v_var, 1)
                largest_h()
                if on(b1) or on(b2) or on(b3):
                    dve.wait_ge(g_rstd, t)
                for k, (n, dst, sem) in enumerate(((b1, x1, v_x1), (b2, x2, v_x2), (b3, x3, v_x3))):
                    if on(n):
                        if k == 0:
                            since(dve, p_x1T, n - 1)
                        if k == 2:
                            since(dve, stored, 16 * n)
                        dve.tensor_scalar(dst[q], y[k], moments[:, k, 0:1], rstd[:, k:k + 1],
                                          ALU.subtract, ALU.mult).then_inc(sem, 1)
                if p == 1 and on(i, BATCH):
                    rest_of_B(i, 0)
                scale_h()
                if p == 1 and on(i, BATCH):
                    rest_of_B(i, 1)
                scale_x2()

            def rest_of_B(b, half):
                dve.wait_ge((a_e0, a_e1)[half], 2 * b + 1)
                dve.tensor_tensor(B_sb[:, 1, half, :], wide[1 + half][:], B_sb[:, 0, half, :],
                                  ALU.subtract).then_inc((v_b0, v_b1)[half], 1)

            chain = [0]

            def link(ins):
                chain[0] += 1
                ins.then_inc(c_chain, 1)
                dve.wait_ge(c_chain, chain[0])

            def atanh_weights():
                dve.wait_ge(pre_sum, 1)
                mean, one_m, ratio, ln_in, ln_out = (prep[:, k, :] for k in (1, 2, 3, 4, 5))
                sq_, acc, small_s, low = (prep[:, k, :] for k in (6, 7, 8, 9))
                dve.tensor_scalar(mean, small[0][:, 0:3], 1.0 / (D * FF), None, ALU.mult
                                  ).then_inc(c_mean, 1)
                dve.wait_ge(c_mean, 1)
                link(dve.tensor_scalar(one_m, mean, -1.0, 1.0, ALU.mult, ALU.add))
                link(dve.reciprocal(ratio, one_m))
                link(dve.scalar_tensor_tensor(ln_in, mean, 1.0, ratio, ALU.add, ALU.mult))
                dve.tensor_tensor(sq_, mean, mean, ALU.mult).then_inc(pre_lnin, 1)
                dve.wait_ge(pre_lnin, 1)
                link(dve.tensor_scalar(acc, sq_, 1.0 / 17.0, None, ALU.mult))
                for k in (15, 13, 11, 9, 7, 5, 3):
                    link(dve.scalar_tensor_tensor(acc, acc, 1.0 / k, sq_, ALU.add, ALU.mult))
                link(dve.scalar_tensor_tensor(acc, acc, 1.0, mean, ALU.add, ALU.mult))
                link(dve.tensor_scalar(low, mean, 0.25, None, ALU.is_lt))
                dve.wait_ge(pre_ln, 1)
                link(dve.tensor_scalar(small_s, ln_out, 0.5, None, ALU.mult))
                link(dve.tensor_tensor(acc, acc, small_s, ALU.subtract))
                link(dve.tensor_tensor(acc, acc, low, ALU.mult))
                link(dve.tensor_tensor(acc, acc, small_s, ALU.add))
                link(dve.tensor_scalar(atanh_q[:], acc, 1.0 / QMAX, None, ALU.mult))
                link(dve.tensor_scalar(small_s, mean, RMS_EPS, HALF_ATANH, ALU.add, ALU.mult))
                link(dve.tensor_scalar(low, small_s, -1.0, None, ALU.mult))

            def ternary_weights():
                flat = "p a b -> p (a b)"
                for w, (raw, dst) in enumerate((
                        (w12_raw[0].rearrange("p b k t -> p (b k t)"),
                         tern12[:, 0].rearrange(flat)),
                        (w12_raw[1].rearrange(flat), tern12[:, 1].rearrange(flat)),
                        (w3_raw.rearrange(flat), tern3[:].rearrange(flat)))):
                    link(dve.tensor_scalar(dst, raw, prep[:, 9, w:w + 1], None, ALU.is_lt))
                    dve.scalar_tensor_tensor(dst, raw, prep[:, 8, w:w + 1], dst, ALU.is_gt,
                                             ALU.subtract).then_inc(c_tern, 1)

            def rope():
                dve.wait_ge(ld_ctx, 16 * 2)
                ctx3 = [ctx_raw[:, r, :].rearrange("p (b l) -> p b l", b=BATCH) for r in range(2)]
                for r in range(2):
                    table = rope_sb[:, r:r + 1, :].to_broadcast([P, BATCH, L])
                    link(dve.tensor_tensor(ctx3[r], ctx3[r], table, ALU.mult))
                dve.wait_ge(c_zero, 3)
                for e in range(2):
                    r = slice(e * L, (e + 1) * L)
                    dve.tensor_tensor(kv_bd[r, :, e * L:(e + 1) * L], ctx3[0][r], ctx3[1][r],
                                      ALU.add).then_inc(c_kv, 1)

            def output_weights():
                for half in range(2):
                    dve.wait_ge(pre_ev, 6 + half)
                    part = [C_sb[:, s, 4 * half:4 * half + 4, :] for s in range(2)]
                    dve.tensor_tensor(part[1], wide[half][:].rearrange("p (c n) -> p c n", c=4),
                                      part[0], ALU.subtract).then_inc(pre_lo, 1)

            def first_weights():
                rope()
                output_weights()

            link(dve.memset(moments[:], 1.0))
            link(dve.memset(spread[:], 1.0))
            atanh_weights()
            ternary_weights()

            run(dve, slot, {0: first_weights})

        @block.gpsimd
        def _(pool):
            def slot(i, p):
                t = 2 * i + p
                n1, n2, n3, b1, b2, b3, q = t, t - 2, t - 4, t - 1, t - 3, t - 5, 1 - p

                def gain_h():
                    if on(n3):
                        pool.wait_ge(v_h, n3 + 1)
                        since(pool, p_hT, n3)
                        pool.tensor_tensor(hg, hh, g3, ALU.mult).then_inc(g_hg, 1)

                def gain_x2():
                    if on(b2):
                        pool.wait_ge(v_x2, b2 + 1)
                        since(pool, p_xqT, b2)
                        pool.tensor_tensor(xg, x2_of(b2, q).rearrange("p (o d) -> p o d", o=1)
                                           .to_broadcast([P, 2, D]), g12, ALU.mult
                                           ).then_inc(g_xg, 1)
                        pool.wait_ge(v_ms, b2 + 1)
                        pool.tensor_tensor(sqx[:, 2:3], sqx[:, 1:2], minus_half[:, 0:1], ALU.pow
                                           ).then_inc(g_rx, 1)

                def normalise_2():
                    if on(n2):
                        pool.wait_ge(v_rec2, n2 + 1)
                        pool.tensor_tensor(
                            heads(P2_even_odd[p]), heads(P2_even_odd[p]),
                            over_heads(r2[:, 1, :].rearrange("p (h o) -> p h o", o=1)), ALU.mult
                            ).then_inc(g_P2, 1)

                def roots(sem, count):
                    pool.wait_ge(sem, count)
                    pool.tensor_tensor(rstd[:], spread[:], minus_half[:], ALU.pow
                                       ).then_inc(g_rstd, 1)

                if in_tail(t):
                    before = TAIL - 1 + sum(on(u - 3) + 1 for u in range(TAIL, t))
                    if on(b2):
                        before += 1
                        roots(v_var, before)
                        gain_x2()
                    if on(n3):
                        gain_h()
                        roots(v_msh, n3 + 1)
                    roots(v_var, before + 1)
                    return

                if p == 0 and on(i - 1, BATCH):
                    since(pool, p_e1, 2 * i - 2)
                    pool.tensor_copy(kv_now[:], kv_bd[:, i - 1, :]).then_inc(g_kv, 1)
                    pool.tensor_copy(kv_cur[:, 0], kv_bd[:, i - 1, :]).then_inc(g_kv, 1)
                    pool.wait_ge(g_kv, 3 * i - 1)
                    pool.tensor_tensor(kv_cur[:, 1], kv_now[:], kv_cur[:, 0], ALU.subtract
                                       ).then_inc(g_kv, 1)
                if on(b1):
                    since(pool, v_y1, b1)
                    pool.tensor_tensor(xb[:], x_sb[:, b1, :], bo_row[:], ALU.add).then_inc(g_xb, 1)
                if on(n1):
                    pool.wait_ge(v_mask, n1 + 1)
                    pool.tensor_tensor(heads(Ls[:]), heads(Ls[:]), over_heads(m8[:, :, 0:1]),
                                       ALU.subtract).then_inc(g_d1, 1)
                    pool.wait_ge(v_rec1, n1 + 1)
                    pool.tensor_tensor(heads(mask[:]), heads(mask[:]),
                                       over_heads(r1[:, 1, :].rearrange("p (h o) -> p h o", o=1)),
                                       ALU.mult).then_inc(g_mr, 1)
                    pool.wait_ge(g_mr, n1 + 1)
                    pool.wait_ge(a_exp1, n1 + 1)
                    pool.tensor_tensor(Ls[:], Ls[:], mask[:], ALU.mult).then_inc(g_P1, 1)
                if in_tail(t, TAIL - 1):
                    normalise_2(), gain_h()
                else:
                    gain_h()
                if on(b1) or on(b2) or on(b3):
                    roots(v_var, t)
                gain_x2()
                if not in_tail(t, TAIL - 1):
                    normalise_2()

            pool.memset(lat_k[:], 0.0).then_inc(c_zero, 1)
            pool.memset(lat_v[:], 0.0).then_inc(c_zero, 1)
            pool.memset(kv_bd[:], 0.0).then_inc(c_zero, 1)
            pool.memset(ident[:], 0.0).then_inc(c_const, 1)
            pool.memset(ones[:], 1.0).then_inc(c_const, 1)
            pool.memset(minus_half[:], -0.5).then_inc(c_const, 1)
            pool.wait_ge(c_const, 3)
            pool.affine_select(out=ident[:], in_=ident[:], compare_op=ALU.not_equal, fill=1.0,
                               base=0, pattern=[[-1, P]], channel_multiplier=1).then_inc(c_ident, 1)

            def first_loads():
                pool.wait_ge(ld_x, 16 * 2)
                pool.wait_ge(ld_back, 16 * 3)

            def rope_made():
                pool.wait_ge(c_kv, 2)

            def gains_loaded():
                pool.wait_ge(ld_g, 16 * 3)

            run(pool, slot, {0: first_loads, 1: rope_made, 2: gains_loaded})


def rope_tables():
    inv_freq = (1.0 / (10000.0 ** (np.arange(0, DC, 2, dtype=np.float32) / np.float32(DC))
                       .astype(np.float32))).astype(np.float32)
    freqs = np.arange(L, dtype=np.float32)[:, None] * inv_freq[None, :]
    sin = np.repeat(np.sin(freqs.astype(np.float64)), 2, axis=-1).astype(np.float32)
    cos = np.repeat(np.cos(freqs.astype(np.float64)), 2, axis=-1).astype(np.float32)
    sin[:, :DC // 2] = -sin[:, :DC // 2]
    return np.ascontiguousarray(np.stack([np.tile(cos.T, (2, 1)), np.tile(sin.T, (2, 1))], axis=1))


def layouts(v):
    x = v["x"]
    ctx = v["ctx_512"].reshape(BATCH * L, DC).T
    rot = np.concatenate([ctx[DC // 2:], ctx[:DC // 2]])

    def chunked(w):
        return w.reshape(-1, P, w.shape[1]).transpose(1, 0, 2)

    lat = v["L0_attn_latent_keys"]
    return {
        "x": x.reshape(TILES, P, D).transpose(1, 0, 2),
        "xT": x.reshape(BATCH, SEQ, KD, P).transpose(3, 0, 2, 1),
        "wqT1": chunked(v["L0_attn_Wq"].T), "wvT1": chunked(v["L0_attn_Wv"].T),
        "woT1": chunked(v["L0_attn_Wo"].T),
        "bqv": np.stack([v["L0_attn_bq"].reshape(KD, P).T, v["L0_attn_bv"].reshape(KD, P).T], 1),
        "bo": v["L0_attn_bo"].reshape(1, D),
        "latT": chunked(lat.T), "lat": lat.reshape(L, PAIRS, 2, HD),
        "ctxT": np.tile(np.stack([ctx, rot], 1), (2, 1, 1)),
        "wkrT": v["L0_xattn_W_kr"].transpose(2, 0, 1),
        "wqrT": v["L0_xattn_W_qr"].transpose(2, 0, 1),
        "wkcqT": v["L0_xattn_w_kc_q"].transpose(2, 0, 1),
        "wqx": v["L0_xattn_Wq"].reshape(H, HK, D).transpose(1, 0, 2),
        "wkckv": v["L0_xattn_w_kc_kv"].transpose(1, 0, 2),
        "woTx": v["L0_xattn_Wo"].T.reshape(H, HK, D).transpose(1, 0, 2),
        "w1T": chunked(v["L0_ffn_w1"].T).reshape(P, -1),
        "w2T": chunked(v["L0_ffn_w2"].T).reshape(P, -1),
        "w3T": chunked(v["L0_ffn_w3"].T),
        "g1": v["L0_ffn_g1"].reshape(1, D), "g2": v["L0_ffn_g2"].reshape(1, D),
        "g3": v["L0_ffn_g3"].reshape(1, FF),
        "rope": rope_tables(),
    }


def kernel(**inputs):
    import concourse.bacc as bacc
    from concourse.bass_utils import run_bass_kernel_spmd

    nc = bacc.Bacc("TRN2", target_bir_lowering=False, num_devices=1)
    arrays, args = {}, {}
    for name, value in layouts({k: np.asarray(v) for k, v in inputs.items()}).items():
        value = np.ascontiguousarray(value)
        arrays[f"in_{name}"] = value
        args[name] = nc.dram_tensor(f"in_{name}", value.shape, mybir.dt.from_np(value.dtype),
                                    kind="ExternalInput").ap()
    out = nc.dram_tensor("out_x", (TILES, P, D), F32, kind="ExternalOutput").ap()
    decoder_layer(nc, args, out)
    r = run_bass_kernel_spmd(nc, [arrays], core_ids=[0])
    return r.results[0]["out_x"].reshape(BATCH, SEQ, D)
```
